# Optimizing a Trainium2 kernel written in Bass

```python
import numpy as np
import jax
import jax.numpy as jnp

def _softmax(x, axis=-1):
    return jax.nn.softmax(x, axis=axis)

def _gelu(x):
    return jax.nn.gelu(x, approximate=True)

def _silu(x):
    return jax.nn.silu(x)

def _sigmoid(x):
    return jax.nn.sigmoid(x)

def _layernorm(x, axis=-1, eps=1e-05):
    m = jnp.mean(x, axis=axis, keepdims=True)
    v = jnp.var(x, axis=axis, keepdims=True)
    return (x - m) / jnp.sqrt(v + eps)

def _scatter_add(tgt, idx, src, axis=0):
    return tgt.at[idx].add(src)

def _segment_sum(src, seg, n):
    return jax.ops.segment_sum(src, seg, n)
kernel_name = 'mk_flamingo_gated_d2_seqx_r4_f0930c'

def setup_inputs(seed: int=0):
    np.random.seed(seed)
    _w = jnp.asarray

    def _rec_inputs():
        import jax
        import jax.numpy as jnp
        _rk = jax.random.key(seed)
        x = -0.0002928 + 1 * jax.random.normal(jax.random.fold_in(_rk, 1), (8, 256, 256), jnp.float32)
        _lenS = 256 - jax.random.randint(jax.random.fold_in(_rk, 7), (8,), 0, max(1, 256 // 4) + 1, jnp.int32)
        _lenS2 = 77 - jax.random.randint(jax.random.fold_in(_rk, 8), (8,), 0, max(1, 77 // 4) + 1, jnp.int32)
        _ctx_1024P = jax.random.normal(jax.random.fold_in(_rk, 11), (8, 16, 256), jnp.float32)
        _ctx_1024c = jax.random.dirichlet(jax.random.fold_in(_rk, 511), 0.3 * jnp.ones((16,), jnp.float32), (8, 77))
        _ctx_1024t = jnp.einsum('bsk,bkd->bsd', _ctx_1024c, _ctx_1024P)
        _ctx_1024t = _ctx_1024t * jax.lax.rsqrt(jnp.mean(jnp.square(_ctx_1024t)) + 1e-12) * 0.953939
        ctx_1024 = 4.13588e-05 + 0.999923 * (_ctx_1024t + 0.3 * jax.random.normal(jax.random.fold_in(_rk, 611), (8, 77, 256), jnp.float32))
        _g = jax.random.normal(jax.random.fold_in(_rk, 9001), (2, 2), jnp.float32)
        _g = jnp.sign(_g) * jnp.maximum(jnp.abs(_g), 1.0) + (_g == 0) * 1.0
        g_xattn = _g[0]
        g_ffn = _g[1]
        return (x, ctx_1024, g_xattn, g_ffn)
    x, ctx_1024, g_xattn, g_ffn = _rec_inputs()

    def _L0_xattn_setup():
        import jax, jax.numpy as jnp
        import numpy as np
        HIDDEN = 256
        N_HEADS = 16
        HEAD_DIM = HIDDEN // N_HEADS
        SCALE = HEAD_DIM ** (-0.5)
        B, QL, KVL = (2, 512, 1024)
        key = jax.random.key(seed)
        ks = jax.random.split(key, 7)
        s = 0.02
        return {'query_states': jax.random.normal(ks[0], (B, QL, HIDDEN), jnp.float32), 'key_states': jax.random.normal(ks[1], (B, KVL, HIDDEN), jnp.float32), 'value_states': jax.random.normal(ks[2], (B, KVL, HIDDEN), jnp.float32), 'Wq': jax.random.normal(ks[3], (HIDDEN, HIDDEN), jnp.float32) * s, 'Wk': jax.random.normal(ks[4], (HIDDEN, HIDDEN), jnp.float32) * s, 'Wv': jax.random.normal(ks[5], (HIDDEN, HIDDEN), jnp.float32) * s, 'Wo': jax.random.normal(ks[6], (HIDDEN, HIDDEN), jnp.float32) * s}
    _L0_xattn_all = _L0_xattn_setup()
    _L0_xattn_in = {k: v for k, v in _L0_xattn_all.items() if k in ('Wq', 'Wk', 'Wv', 'Wo')}
    del _L0_xattn_all

    def _L0_ffn_setup():
        import jax, jax.numpy as jnp
        import numpy as np
        EPS = 1e-05

        def rmsnorm(x):
            return x * jax.lax.rsqrt(jnp.mean(x * x, axis=-1, keepdims=True) + EPS)

        def act_quant(x):
            scale = 127.0 / jnp.clip(jnp.max(jnp.abs(x), axis=-1, keepdims=True), 1e-05)
            q = jnp.clip(jnp.round(x * scale), -128.0, 127.0) / scale
            return x + jax.lax.stop_gradient(q - x)

        def weight_quant(w):
            scale = 1.0 / jnp.clip(jnp.mean(jnp.abs(w)), 1e-05)
            q = jnp.clip(jnp.round(w * scale), -1.0, 1.0) / scale
            return w + jax.lax.stop_gradient(q - w)

        def bitlinear(x, w, b):
            xq = act_quant(rmsnorm(x))
            wq = weight_quant(w)
            return jnp.einsum('bsd,fd->bsf', xq, wq) + b
        key = jax.random.key(seed)
        k0, k1, k2 = jax.random.split(key, 3)
        B, S, D, F = (2, 2048, 256, 1024)
        x = jax.random.normal(k0, (B, S, D), dtype=jnp.float32)
        w1 = jax.random.normal(k1, (F, D), dtype=jnp.float32) * (1.0 / np.sqrt(D))
        b1 = jnp.zeros((F,), dtype=jnp.float32)
        w2 = jax.random.normal(k2, (D, F), dtype=jnp.float32) * (1.0 / np.sqrt(F))
        b2 = jnp.zeros((D,), dtype=jnp.float32)
        return {'x': x, 'w1': w1, 'b1': b1, 'w2': w2, 'b2': b2}
    _L0_ffn_all = _L0_ffn_setup()
    _L0_ffn_in = {k: v for k, v in _L0_ffn_all.items() if k in ('w1', 'b1', 'w2', 'b2')}
    del _L0_ffn_all

    def _L1_xattn_setup():
        import jax, jax.numpy as jnp
        import numpy as np
        N_EMBD = 256
        N_HEAD = 16
        DIM_HEAD = N_EMBD // N_HEAD
        SCALE = DIM_HEAD ** (-0.5)
        key = jax.random.key(seed)
        k1, k2, k3, k4, k5 = jax.random.split(key, 5)
        B, Tq, Tkv = (2, 512, 512)
        x_q = jax.random.normal(k1, (B, Tq, N_EMBD), dtype=jnp.float32)
        x_kv = jax.random.normal(k2, (B, Tkv, N_EMBD), dtype=jnp.float32)
        s = 0.02
        W_q = jax.random.normal(k3, (N_EMBD, N_EMBD), dtype=jnp.float32) * s
        W_kv = jax.random.normal(k4, (N_EMBD, 2 * N_EMBD), dtype=jnp.float32) * s
        W_proj = jax.random.normal(k5, (N_EMBD, N_EMBD), dtype=jnp.float32) * s
        return {'x_q': x_q, 'x_kv': x_kv, 'W_q': W_q, 'W_kv': W_kv, 'W_proj': W_proj}
    _L1_xattn_all = _L1_xattn_setup()
    _L1_xattn_in = {k: v for k, v in _L1_xattn_all.items() if k in ('W_q', 'W_kv', 'W_proj')}
    del _L1_xattn_all

    def _L1_ffn_setup():
        import jax, jax.numpy as jnp
        import numpy as np
        B, S, D, E = (2, 512, 256, 8)
        key = jax.random.key(seed)
        ks = jax.random.split(key, 5)
        x = jax.random.normal(ks[0], (B, S, D), dtype=jnp.float32)
        router_w = jax.random.normal(ks[1], (E, D), dtype=jnp.float32) * 0.02
        router_b = jnp.zeros((E,), dtype=jnp.float32)
        expert_w = jax.random.normal(ks[2], (E, D, D), dtype=jnp.float32) * 0.02
        expert_b = jnp.zeros((E, D), dtype=jnp.float32)
        return {'x': x, 'router_w': router_w, 'router_b': router_b, 'expert_w': expert_w, 'expert_b': expert_b}
    _L1_ffn_all = _L1_ffn_setup()
    _L1_ffn_in = {k: v for k, v in _L1_ffn_all.items() if k in ('router_w', 'router_b', 'expert_w', 'expert_b')}
    del _L1_ffn_all
    return {'x': x, 'ctx_1024': ctx_1024, 'g_xattn': g_xattn, 'g_ffn': g_ffn, 'L0_xattn_Wq': _L0_xattn_in['Wq'], 'L0_xattn_Wk': _L0_xattn_in['Wk'], 'L0_xattn_Wv': _L0_xattn_in['Wv'], 'L0_xattn_Wo': _L0_xattn_in['Wo'], 'L0_ffn_w1': _L0_ffn_in['w1'], 'L0_ffn_b1': _L0_ffn_in['b1'], 'L0_ffn_w2': _L0_ffn_in['w2'], 'L0_ffn_b2': _L0_ffn_in['b2'], 'L1_xattn_W_q': _L1_xattn_in['W_q'], 'L1_xattn_W_kv': _L1_xattn_in['W_kv'], 'L1_xattn_W_proj': _L1_xattn_in['W_proj'], 'L1_ffn_router_w': _L1_ffn_in['router_w'], 'L1_ffn_router_b': _L1_ffn_in['router_b'], 'L1_ffn_expert_w': _L1_ffn_in['expert_w'], 'L1_ffn_expert_b': _L1_ffn_in['expert_b']}

def reference(x, ctx_1024, g_xattn, g_ffn, L0_xattn_Wq, L0_xattn_Wk, L0_xattn_Wv, L0_xattn_Wo, L0_ffn_w1, L0_ffn_b1, L0_ffn_w2, L0_ffn_b2, L1_xattn_W_q, L1_xattn_W_kv, L1_xattn_W_proj, L1_ffn_router_w, L1_ffn_router_b, L1_ffn_expert_w, L1_ffn_expert_b):
    import jax
    import jax.numpy as jnp

    def _L0_xattn_ref(query_states, key_states, value_states, Wq, Wk, Wv, Wo):
        import jax, jax.numpy as jnp
        import numpy as np
        HIDDEN = 256
        N_HEADS = 16
        HEAD_DIM = HIDDEN // N_HEADS
        SCALE = HEAD_DIM ** (-0.5)
        B, QL, KVL = (2, 512, 1024)
        b, ql, _ = query_states.shape
        kvl = key_states.shape[1]
        q = query_states @ Wq.T
        k = key_states @ Wk.T
        v = value_states @ Wv.T
        q = q.reshape(b, ql, N_HEADS, HEAD_DIM).transpose(0, 2, 1, 3)
        k = k.reshape(b, kvl, N_HEADS, HEAD_DIM).transpose(0, 2, 1, 3)
        v = v.reshape(b, kvl, N_HEADS, HEAD_DIM).transpose(0, 2, 1, 3)
        scores = jnp.einsum('bhqd,bhkd->bhqk', q, k) * SCALE
        attn = jax.nn.softmax(scores, axis=-1)
        out = jnp.einsum('bhqk,bhkd->bhqd', attn, v)
        out = out.transpose(0, 2, 1, 3).reshape(b, ql, HIDDEN)
        return out @ Wo.T

    def _L0_ffn_ref(x, w1, b1, w2, b2):
        import jax, jax.numpy as jnp
        import numpy as np
        EPS = 1e-05

        def rmsnorm(x):
            return x * jax.lax.rsqrt(jnp.mean(x * x, axis=-1, keepdims=True) + EPS)

        def act_quant(x):
            scale = 127.0 / jnp.clip(jnp.max(jnp.abs(x), axis=-1, keepdims=True), 1e-05)
            q = jnp.clip(jnp.round(x * scale), -128.0, 127.0) / scale
            return x + jax.lax.stop_gradient(q - x)

        def weight_quant(w):
            scale = 1.0 / jnp.clip(jnp.mean(jnp.abs(w)), 1e-05)
            q = jnp.clip(jnp.round(w * scale), -1.0, 1.0) / scale
            return w + jax.lax.stop_gradient(q - w)

        def bitlinear(x, w, b):
            xq = act_quant(rmsnorm(x))
            wq = weight_quant(w)
            return jnp.einsum('bsd,fd->bsf', xq, wq) + b
        h = bitlinear(x, w1, b1)
        h = jax.nn.gelu(h, approximate=False)
        return bitlinear(h, w2, b2)

    def _L1_xattn_ref(x_q, x_kv, W_q, W_kv, W_proj):
        import jax, jax.numpy as jnp
        import numpy as np
        N_EMBD = 256
        N_HEAD = 16
        DIM_HEAD = N_EMBD // N_HEAD
        SCALE = DIM_HEAD ** (-0.5)
        B, Tq, C = x_q.shape
        Tkv = x_kv.shape[1]
        q = x_q @ W_q
        kv = x_kv @ W_kv
        k, v = jnp.split(kv, 2, axis=2)
        q = q.reshape(B, Tq, N_HEAD, DIM_HEAD).transpose(0, 2, 1, 3)
        k = k.reshape(B, Tkv, N_HEAD, DIM_HEAD).transpose(0, 2, 1, 3)
        v = v.reshape(B, Tkv, N_HEAD, DIM_HEAD).transpose(0, 2, 1, 3)
        attn = jnp.einsum('bhqd,bhkd->bhqk', q, k) / SCALE
        attn = jax.nn.softmax(attn, axis=-1)
        y = jnp.einsum('bhqk,bhkd->bhqd', attn, v)
        y = y.transpose(0, 2, 1, 3).reshape(B, Tq, C)
        return y @ W_proj

    def _L1_ffn_ref(x, router_w, router_b, expert_w, expert_b):
        import jax, jax.numpy as jnp
        import numpy as np
        B, S, D, E = (2, 512, 256, 8)
        logits = jnp.einsum('bsd,ed->bse', x, router_w) + router_b
        probs = jax.nn.softmax(logits, axis=-1)
        weights = jnp.max(probs, axis=-1)
        top1 = jnp.argmax(probs, axis=-1)
        y_all = jnp.einsum('bsd,eod->bseo', x, expert_w) + expert_b
        y = jnp.take_along_axis(y_all, top1[:, :, None, None], axis=2)[:, :, 0, :]
        out = y * weights[:, :, None]
        return out
    x = x + jnp.tanh(g_xattn[0]) * _L0_xattn_ref(_layernorm(x, axis=-1), ctx_1024, ctx_1024, L0_xattn_Wq, L0_xattn_Wk, L0_xattn_Wv, L0_xattn_Wo)
    x = x + jnp.tanh(g_ffn[0]) * _L0_ffn_ref(_layernorm(x, axis=-1), L0_ffn_w1, L0_ffn_b1, L0_ffn_w2, L0_ffn_b2)
    x = x + jnp.tanh(g_xattn[1]) * _L1_xattn_ref(_layernorm(x, axis=-1), ctx_1024, L1_xattn_W_q, L1_xattn_W_kv, L1_xattn_W_proj)
    x = x + jnp.tanh(g_ffn[1]) * _L1_ffn_ref(_layernorm(x, axis=-1), L1_ffn_router_w, L1_ffn_router_b, L1_ffn_expert_w, L1_ffn_expert_b)
    return x

_drawn_inputs = setup_inputs


def setup_inputs(seed=0):
    import zlib

    import numpy as np

    out = dict(_drawn_inputs(seed))
    spreads = {'g_ffn': (-1.0, 0.6),
     'L0_ffn_b1': (0.0, 0.1),
     'L0_ffn_b2': (0.0, 0.1),
     'L1_ffn_router_b': (0.0, 0.1),
     'L1_ffn_expert_b': (0.0, 0.512)}
    factors = {'L0_xattn_Wq': 7.819, 'L0_xattn_Wk': 8.0}
    for name, (base, spread) in spreads.items():
        noise = np.random.default_rng([zlib.crc32(name.encode()), seed]).standard_normal(out[name].shape)
        drawn = base * np.exp(spread * noise) if base else spread * noise
        out[name] = jnp.asarray(drawn.astype(out[name].dtype))
    for name, factor in factors.items():
        out[name] = (out[name] * factor).astype(out[name].dtype)
    return out
```

```python
from contextlib import ExitStack

import concourse.bass as bass
from concourse import mybir

F32 = mybir.dt.float32
F16 = mybir.dt.float16
BF16 = mybir.dt.bfloat16
ALU = mybir.AluOpType
ACT = mybir.ActivationFunctionType
AX = mybir.AxisListType

P = 128
B, S, D = 8, 256, 256
T = S // P
C = D // P
KEYS = 77
H, HD = 16, 16
PAIRS = H // 2
F = 1024
FC = F // P
E = 8
HALF = 512
STACK = 3 * 2 * HD
ROWS = STACK + 4
EPS = 1e-5
MAGIC = 12582912.0
WSCALE = 1024.0
SCALES = (0.25, 4.0)


def before(eng, sem, b, per):
    if not (isinstance(b, int) and b == 0):
        eng.wait_ge(sem, b * per)


class Stream:

    def __init__(self, ctx, nc, name, layer, probs=None):
        def sb(n, shape, dt=F32):
            return ctx.enter_context(nc.sbuf_tensor(f"{name}_{n}", shape, dt))

        def sem(n):
            return ctx.enter_context(nc.semaphore(f"{name}_{n}"))

        self.layer = layer
        self.scale = SCALES[layer]
        self.wide = [ctx.enter_context(nc.psum_tensor(f"{name}_wide{i}", [P, HALF], F32)) for i in range(2)]
        self.bank_a = ctx.enter_context(nc.psum_tensor(f"{name}_bank_a", [P, HALF], F32))
        self.bank_b = ctx.enter_context(nc.psum_tensor(f"{name}_bank_b", [P, HALF], F32))
        self.x_in = sb("x_in", [P, T, D])
        self.ctx_in = sb("ctx_in", [KEYS, D])
        self.stats = sb("stats", [P, T, 6])
        self.mean_var = sb("mean_var", [P, T, 2])
        self.rstd = sb("rstd", [P, T])
        self.xn = sb("xn", [P, T, D])
        self.xnT = sb("xnT", [P, C, S])
        self.ctxT = sb("ctxT", [P, C, KEYS])
        self.q_parts = sb("q_parts", [P, 2, C, S], F16)
        self.k_parts = sb("k_parts", [P, 2, C, KEYS], F16)
        self.q_stack = sb("q_stack", [ROWS, PAIRS, S], F16)
        self.k_pairs = sb("k_pairs", [ROWS, PAIRS, KEYS], F16)
        self.k_stack = sb("k_stack", [ROWS, PAIRS, 2, KEYS], F16)
        self.v_cols = sb("v_cols", [KEYS, PAIRS, 2, 2 * HD])
        self.neg_max = sb("neg_max", [P, T, H])
        self.max_parts = sb("max_parts", [P, T, 2, 2, PAIRS], F16)
        self.maxT = sb("maxT", [2 * H, S], F16)
        self.probs = sb("probs", [KEYS, H, S]) if probs is None else probs
        self.den_inv = sb("den_inv", [P, C, S])
        self.heads_out = sb("heads_out", [P, C, S])
        self.x_attn = sb("x_attn", [P, T, D])
        self.q_dram = nc.dram_tensor(f"{name}_q_dram", [2, D, S], F16, kind="Internal").ap()
        self.k_dram = nc.dram_tensor(f"{name}_k_dram", [2, D, KEYS], F16, kind="Internal").ap()
        self.max_dram = nc.dram_tensor(f"{name}_max_dram", [2 * H, S], F16, kind="Internal").ap()
        self.x_ready = sem("x_ready")
        self.ctx_ready = sem("ctx_ready")
        self.stats_ready = sem("stats_ready")
        self.xn_ready = sem("xn_ready")
        self.xnT_psum = sem("xnT_psum")
        self.xnT_ready = sem("xnT_ready")
        self.ctxT_psum = sem("ctxT_psum")
        self.ctxT_ready = sem("ctxT_ready")
        self.q_psum = sem("q_psum")
        self.k_psum = sem("k_psum")
        self.v_psum = sem("v_psum")
        self.q_high = sem("q_high")
        self.q_low = sem("q_low")
        self.k_high = sem("k_high")
        self.k_low = sem("k_low")
        self.v_ready = sem("v_ready")
        self.q_stored = sem("q_stored")
        self.k_stored = sem("k_stored")
        self.q_stacked = sem("q_stacked")
        self.k_paired = sem("k_paired")
        self.k_stacked = sem("k_stacked")
        self.scores_psum = sem("scores_psum")
        self.max_ready = sem("max_ready")
        self.max_high = sem("max_high")
        self.max_low = sem("max_low")
        self.maxT_psum = sem("maxT_psum")
        self.maxT_ready = sem("maxT_ready")
        self.max_stored = sem("max_stored")
        self.max_stacked = sem("max_stacked")
        self.shifted_psum = sem("shifted_psum")
        self.probs_ready = sem("probs_ready")
        self.heads_psum = sem("heads_psum")
        self.den_ready = sem("den_ready")
        self.heads_ready = sem("heads_ready")
        self.attn_psum = sem("attn_psum")
        self.x_attn_ready = sem("x_attn_ready")
        self.ln2_stats = sem("ln2_stats")
        self.xn2_ready = sem("xn2_ready")
        self.xn2T_psum = sem("xn2T_psum")
        self.mean_var2 = sb("mean_var2", [P, T, 2])
        self.rstd2 = sb("rstd2", [P, T])
        self.xn2 = sb("xn2", [P, T, D])


def flamingo_kernel(nc, x, ctx_tokens, g_xattn, g_ffn, wq0, wk0, wv0, wo0, w1, b1, w2, b2,
                    wq1, wkv1, wproj1, router_w, router_b, expert_w, expert_b, consts, out):
    ctx = ExitStack()
    with ctx:
        def sb(n, shape, dt=F32):
            return ctx.enter_context(nc.sbuf_tensor(n, shape, dt))

        def sem(n):
            return ctx.enter_context(nc.semaphore(n))

        X = Stream(ctx, nc, "x", 0)
        ew_nat = sb("ew_nat", [P, E, C, D])
        Y = Stream(ctx, nc, "y", 1, ew_nat[0:KEYS, :, :, :].rearrange("p e k d -> p (e k) d"))

        cst = sb("cst", [P, P + 2 + E])
        ident = cst[:, 0:P]
        head_mask = cst[:, P:P + 2]
        rank = cst[:, P + 2:P + 2 + E]
        ident16 = sb("ident16", [P, P], F16)
        identb = sb("identb", [P, P], BF16)
        ones = sb("ones", [P, P])
        minus_half = sb("minus_half", [P, T])
        eps = sb("eps", [P, T])
        stats_seen = sb("stats_seen", [P, 1])
        ones_head = sb("ones_head", [KEYS, 2, 2 * HD])
        gates = sb("gates", [P, 4])
        nat = [sb(f"nat{i}", [P, C, D]) for i in range(4)]
        wT = [sb(f"wT{i}", [P, C, D]) for i in range(4)]
        wq1_sb = sb("wq1_sb", [P, C, D])
        wkv1_sb = sb("wkv1_sb", [P, C, 2 * D])
        wproj1_sb = sb("wproj1_sb", [P, C, D])
        w12 = sb("w12", [P, 2, FC * D])
        w12_r = sb("w12_r", [P, 2, FC * D])
        w12_t = sb("w12_t", [P, 2, FC * D], BF16)
        w1T = sb("w1T", [P, C, F], BF16)
        w2T = sb("w2T", [P, FC, D], BF16)
        abs_sum = sb("abs_sum", [P, 2])
        w_mean = sb("w_mean", [P, 2])
        w_inv = sb("w_inv", [P, 2])
        w_deq = sb("w_deq", [P, 2])
        gate_b2 = sb("gate_b2", [P, D])
        b1_sb = sb("b1_sb", [P, F])
        b2_sb = sb("b2_sb", [P, D])
        ew_high = sb("ew_high", [P, C, E, D], F16)
        ew_low = sb("ew_low", [P, C, E, D], F16)
        rw_nat = sb("rw_nat", [E, D])
        rwT = sb("rwT", [P, C, E])
        rb_sb = sb("rb_sb", [1, E])
        eb_sb = sb("eb_sb", [E, D])
        absmax = sb("absmax", [P, T])
        ffs = sb("ffs", [P, 8, T])
        xm = sb("xm", [P, T, D])
        xqT = sb("xqT", [P, C, S], BF16)
        hid = w12_r[:, 0, :].rearrange("p (t f) -> p t f", t=T)
        gel = w12_r[:, 1, :].rearrange("p (t f) -> p t f", t=T)
        sumsq = sb("sumsq", [P, T])
        hmax = sb("hmax", [P, T])
        hm = w12[:, 0, :].rearrange("p (t f) -> p t f", t=T)
        hq = w12_t[:, 0, :].rearrange("p (t f) -> p t f", t=T)
        hqT = w12_t[:, 1, :].rearrange("p (t f s) -> p t f s", t=T, f=FC)
        x1b = nat[3]
        xe = nat[2]
        xe_parts = sb("xe_parts", [P, 2, C, S], F16)
        logits = sb("logits", [P, T, E])
        lmax = sb("lmax", [P, T])
        ldiff = sb("ldiff", [P, T, E])
        lexp = sb("lexp", [P, T, E])
        lsum = sb("lsum", [P, T])
        weight = sb("weight", [P, T])
        tie = sb("tie", [P, T, E])
        tmax = sb("tmax", [P, T])
        hot = sb("hot", [P, T, E])
        mix = sb("mix", [P, T, E])
        mix_w = sb("mix_w", [P, T, E])
        mixT = sb("mixT", [E, T, P])
        acc = nat[0:2]

        s_cst, s_attn_w, s_small, s_w12, s_w1y, s_exp = (
            sem(n) for n in ("cst_loaded", "attn_w_loaded", "small_loaded", "w12_loaded", "layer1_loaded",
                             "experts_loaded"))
        s_ident = sem("ident_ready")
        s_rows = sem("max_rows_ready")
        s_gated = sem("ffn_scale_gated")
        s_zero = sem("zeroed")
        s_pad = sem("padding_ready")
        s_gate = sem("gates_ready")
        s_prep = sem("prep_psum")
        s_prep_act = sem("prep_evicted")
        s_prep_low = sem("prep_low")
        s_abs = sem("abs_summed")
        s_tern = sem("ternary_steps")
        s_absmax, s_ffs, s_xm, s_xqT = (sem(n) for n in ("absmax_ready", "ffs_steps", "xm_ready", "xqT_ready"))
        s_h_psum, s_hid, s_gel, s_sumsq, s_hmax, s_hs = (
            sem(n) for n in ("h_psum", "hid_ready", "gelu_ready", "sumsq_ready", "hmax_ready", "h_scale_steps"))
        s_hm, s_hq, s_hqT_psum, s_hqT, s_y_psum, s_x1b = (
            sem(n) for n in ("hm_ready", "hq_ready", "hqT_psum", "hqT_ready", "ffn_psum", "x1b_ready"))
        s_xe, s_xe_high, s_xe_low, s_router, s_route, s_lexp = (
            sem(n) for n in ("xe_ready", "xe_high", "xe_low", "router_psum", "route_steps", "lexp_ready"))
        s_mixT_psum, s_mixT, s_bias_psum, s_exp_psum, s_acc, s_out = (
            sem(n) for n in ("mixT_psum", "mixT_ready", "bias_psum", "expert_psum", "acc_steps", "out_stored"))

        weights = {0: (wT[0], wT[1][:, :, :], wT[2][:, :, :], wT[3]),
                   1: (wq1_sb, wkv1_sb[:, :, 0:D], wkv1_sb[:, :, D:2 * D], wproj1_sb)}

        PREP_BANKS = [Y.wide[0], Y.wide[1], Y.bank_a, Y.bank_b]
        LN_STEPS = 2 * T + 2
        FFS_STEPS = 9
        HS_STEPS = 7
        ROUTE_STEPS = 10
        ACC_STEPS = T * (E + 1)

        def prologue(run):
            run("prep_attention", None)
            for stage in ("ln", "qkv"):
                run(stage, X, 0)
            run("prep_ternary", None)
            for stage in ("maxima", "softmax", "attn_out"):
                run(stage, X, 0)
            run("prep_experts", None)
            for stage in ("ffn_in", "ffn_hidden", "ffn_out"):
                run(stage, X, 0)

        BOTH = [("ln", Y), ("qkv", Y), ("ln", X), ("qkv", X), ("maxima", Y), ("maxima", X),
                ("softmax", Y), ("softmax", X), ("attn_out", Y), ("attn_out", X),
                ("route", Y), ("ffn_in", X), ("experts", Y), ("ffn_hidden", X), ("ffn_out", X)]
        LAST = [("ln", Y), ("qkv", Y), ("maxima", Y), ("softmax", Y), ("attn_out", Y),
                ("route", Y), ("experts", Y)]

        def program(eng, run):
            prologue(run)
            for stage, st in BOTH:
                run(stage, st, 1 if st is X else 0)
            with eng.Fori(1, B - 1) as i:
                for stage, st in BOTH:
                    run(stage, st, i + 1 if st is X else i)
            for stage, st in LAST:
                run(stage, st, B - 1)

        def acc_after(n):
            t, g = n // 4, n % 4
            return t * (E + 1) + 1 + 2 * g + 2

        block = ctx.enter_context(nc.Block())

        @block.sync
        def _(sp):
            def load_x(b):
                before(sp, X.x_attn_ready, b, T)
                sp.dma_start(X.x_in[:, :, :], x[b].rearrange("(t p) d -> p t d", p=P)).then_inc(X.x_ready, 16)

            def load_ctx(st, b):
                before(sp, st.ctxT_psum, b, 1)
                sp.dma_start(st.ctx_in[:, :], ctx_tokens[b]).then_inc(st.ctx_ready, 16)

            def natural(dst, src):
                return sp.dma_start(dst, src.rearrange("(k p) n -> p k n", p=P))

            def prep_attention():
                sp.dma_start(cst[:, :], consts).then_inc(s_cst, 16)
                load_x(0)
                load_ctx(X, 0)
                for i, w in enumerate((wq0, wk0, wv0, wo0)):
                    natural(nat[i][:, :, :], w).then_inc(s_attn_w, 16)
                sp.dma_start(gates[:, 0:2], g_xattn.partition_broadcast(P)).then_inc(s_small, 16)
                sp.dma_start(gates[:, 2:4], g_ffn.partition_broadcast(P)).then_inc(s_small, 16)
                sp.dma_start(w12[:, 0, :].rearrange("p (k n) -> p k n", k=FC),
                             w1.rearrange("(k p) n -> p k n", p=P)).then_inc(s_w12, 16)
                sp.dma_start(w12[:, 1, :].rearrange("p (k n) -> p k n", k=C),
                             w2.rearrange("(k p) n -> p k n", p=P)).then_inc(s_w12, 16)
                sp.dma_start(b1_sb[:, :], b1.partition_broadcast(P)).then_inc(s_small, 16)
                sp.dma_start(b2_sb[:, :], b2.partition_broadcast(P)).then_inc(s_small, 16)

            def prep_ternary():
                sp.dma_start(ew_nat[:, :, :, :].rearrange("p e k d -> p (e k) d"),
                             expert_w.rearrange("e (k p) d -> p (e k) d", p=P)).then_inc(s_exp, 16)
                sp.dma_start(rw_nat[:, :], router_w).then_inc(s_exp, 16)

            def prep_experts():
                natural(wq1_sb[:, :, :], wq1).then_inc(s_w1y, 16)
                natural(wkv1_sb[:, :, :], wkv1).then_inc(s_w1y, 16)
                natural(wproj1_sb[:, :, :], wproj1).then_inc(s_w1y, 16)
                sp.dma_start(rb_sb[:, :], router_b.rearrange("(a e) -> a e", a=1)).then_inc(s_w1y, 16)
                sp.dma_start(eb_sb[:, :], expert_b).then_inc(s_w1y, 16)

            def ln(st, b):
                if isinstance(b, int) and b == 0 and st is X:
                    return
                if st is X:
                    load_x(b)
                load_ctx(st, b)

            def qkv(st, b):
                sp.wait_ge(st.k_high, b + 1)
                sp.wait_ge(st.k_low, b + 1)
                sp.dma_start(st.k_dram.rearrange("a (c p) k -> p a c k", p=P),
                             st.k_parts[:, :, :, :]).then_inc(st.k_stored, 16)
                sp.wait_ge(st.q_high, b + 1)
                sp.wait_ge(st.q_low, b + 1)
                sp.dma_start(st.q_dram.rearrange("a (c p) s -> p a c s", p=P),
                             st.q_parts[:, :, :, :]).then_inc(st.q_stored, 16)
                sp.wait_ge(st.k_stored, 16 * (b + 1))
                for n, part in enumerate((0, 0, 1)):
                    sp.dma_start(st.k_pairs[32 * n:32 * n + 32, :, :],
                                 st.k_dram[part].rearrange("(j r) k -> r j k", r=32)).then_inc(st.k_paired, 16)
                sp.wait_ge(st.q_stored, 16 * (b + 1))
                for n, part in enumerate((0, 1, 0)):
                    sp.dma_start(st.q_stack[32 * n:32 * n + 32, :, :],
                                 st.q_dram[part].rearrange("(j r) s -> r j s", r=32)).then_inc(st.q_stacked, 16)

            def maxima(st, b):
                sp.wait_ge(st.maxT_ready, b + 1)
                sp.dma_start(st.max_dram, st.maxT[:, :]).then_inc(st.max_stored, 16)
                sp.wait_ge(st.max_stored, 16 * (b + 1))
                sp.dma_start(st.q_stack[STACK:ROWS, :, :],
                             st.max_dram.rearrange("(r j) s -> r j s", r=4)).then_inc(st.max_stacked, 16)

            def experts(st, b):
                sp.wait_ge(s_acc, b * ACC_STEPS + ACC_STEPS)
                sp.dma_start(out[b].rearrange("(t p) d -> p t d", p=P), acc[0][:, :, :]).then_inc(s_out, 16)

            parts = dict(prep_attention=prep_attention, prep_ternary=prep_ternary, prep_experts=prep_experts,
                         ln=ln, qkv=qkv, maxima=maxima, experts=experts)

            def run(stage, st, b=None):
                if stage in parts:
                    parts[stage](*(() if st is None else (st, b)))

            program(sp, run)
            sp.wait_ge(s_out, 16 * B)

        @block.tensor
        def _(pe):
            def prep_free(n):
                m = n - len(PREP_BANKS)
                if m < 0:
                    return
                if m < 4:
                    pe.wait_ge(s_prep_act, m + 1)
                elif m == 4:
                    pe.wait_ge(s_tern, 1)
                elif m < 10:
                    pe.wait_ge(s_prep_act, m)
                else:
                    pe.wait_ge(s_prep_low, m - 9)

            def prep_attention():
                pe.wait_ge(s_cst, 16)
                pe.wait_ge(s_attn_w, 64)
                for n in range(4):
                    bank = PREP_BANKS[n][:, :].rearrange("p (k o) -> p k o", k=C)
                    for k in range(C):
                        for o in range(C):
                            mm = pe.transpose(bank[:, k, o * P:(o + 1) * P], nat[n][:, o, k * P:(k + 1) * P], ident)
                    mm.then_inc(s_prep, 1)

            def prep_ternary():
                prep_free(4)
                pe.wait_ge(s_abs, 2)
                pe.wait_ge(s_pad, 1)
                pe.matmul(PREP_BANKS[0][:, 0:2], ones[:, :], abs_sum[:, :], start=True, stop=True).then_inc(s_prep, 1)
                pe.wait_ge(s_tern, 7)
                pe.wait_ge(s_ident, 2)
                for n in range(4):
                    prep_free(5 + n)
                    bank = PREP_BANKS[(5 + n) % 4][:, :].bitcast(BF16)
                    for j in range(8):
                        if n < 2:
                            src = w12_t[:, 0, j * D + n * P:j * D + (n + 1) * P]
                        else:
                            f, d = 4 * (n - 2) + j // 2, j % 2
                            src = w12_t[:, 1, d * F + f * P:d * F + (f + 1) * P]
                        mm = pe.transpose(bank[:, j * P:(j + 1) * P], src, identb[:, :])
                    mm.then_inc(s_prep, 1)

            def prep_experts():
                pe.wait_ge(s_exp, 32)
                prep_free(9)
                for k in range(C):
                    mm = pe.transpose(PREP_BANKS[9 % 4][:, k * E:(k + 1) * E], rw_nat[:, k * P:(k + 1) * P],
                                      ident[0:E, 0:E])
                mm.then_inc(s_prep, 1)
                for e in range(E):
                    prep_free(10 + e)
                    bank = PREP_BANKS[(10 + e) % 4][:, :].rearrange("p (k o) -> p k o", k=C)
                    for k in range(C):
                        for o in range(C):
                            mm = pe.transpose(bank[:, k, o * P:(o + 1) * P], ew_nat[:, e, o, k * P:(k + 1) * P], ident)
                    mm.then_inc(s_prep, 1)

            def turn_tokens(dst, src, ready, b):
                for t in range(T):
                    pe.wait_ge(ready, b * T + t + 1)
                    for c in range(C):
                        mm = pe.transpose(dst[:, c, t * P:(t + 1) * P], src[:, t, c * P:(c + 1) * P], ident)
                return mm

            def ln(st, b):
                if st is X:
                    before(pe, s_hqT, b, 2)
                else:
                    before(pe, s_acc, b, ACC_STEPS)
                    if isinstance(b, int) and b == 0:
                        pe.wait_ge(s_prep_act, 9 + E)
                        pe.wait_ge(s_prep_low, E)
                        pe.wait_ge(s_w1y, 80)
                a = st.bank_a[:, :].rearrange("p (c s) -> p c s", c=C)
                turn_tokens(a, st.xn, st.xn_ready, b).then_inc(st.xnT_psum, 1)
                pe.wait_ge(st.ctx_ready, 16 * (b + 1))
                bb = st.bank_b[:, :].rearrange("p (c s) -> p c s", c=C)
                for c in range(C):
                    mm = pe.transpose(bb[:, c, 0:KEYS], st.ctx_in[:, c * P:(c + 1) * P], ident[0:KEYS, 0:KEYS])
                mm.then_inc(st.ctxT_psum, 1)

            def qkv(st, b):
                wq, wk, wv, _ = weights[st.layer]
                a = st.bank_a[:, :].rearrange("p (c s) -> p c s", c=C)
                bb = st.bank_b[:, :].rearrange("p (c s) -> p c s", c=C)
                if st is X and isinstance(b, int) and b == 0:
                    pe.wait_ge(s_prep_act, 4)
                pe.wait_ge(st.ctxT_ready, b + 1)
                for o in range(C):
                    for k in range(C):
                        mm = pe.matmul(bb[:, o, 0:KEYS], wk[:, k, o * P:(o + 1) * P], st.ctxT[:, k, :],
                                       start=(k == 0), stop=(k == C - 1))
                mm.then_inc(st.k_psum, 1)
                if st is X:
                    before(pe, Y.x_ready, b, T)
                for k in range(C):
                    mm = pe.matmul(st.wide[0][0:KEYS, 0:D], st.ctxT[:, k, :], wv[:, k, :],
                                   start=(k == 0), stop=(k == C - 1))
                mm.then_inc(st.v_psum, 1)
                pe.wait_ge(st.xnT_ready, b + 1)
                for o in range(C):
                    for k in range(C):
                        mm = pe.matmul(a[:, o, :], wq[:, k, o * P:(o + 1) * P], st.xnT[:, k, :],
                                       start=(k == 0), stop=(k == C - 1))
                mm.then_inc(st.q_psum, 1)

            def maxima(st, b):
                pe.wait_ge(st.v_ready, 2 * (b + 1))
                pe.wait_ge(st.k_stacked, 2 * (b + 1))
                pe.wait_ge(st.q_stacked, 48 * (b + 1))
                for n in range(8):
                    t, g = n // 4, n % 4
                    if n >= 2:
                        pe.wait_ge(st.max_ready, 8 * b + n - 1)
                    for j in range(2):
                        mm = pe.matmul(st.wide[n % 2][:, j * 2 * KEYS:(j + 1) * 2 * KEYS],
                                       st.q_stack[0:STACK, 2 * g + j, t * P:(t + 1) * P],
                                       st.k_stack[0:STACK, 2 * g + j, :, :].rearrange("p r k -> p (r k)"),
                                       start=True, stop=True)
                    mm.then_inc(st.scores_psum, 1)
                pe.wait_ge(st.max_low, b + 1)
                b16 = st.bank_b[:, :].bitcast(F16)
                for t in range(T):
                    mm = pe.transpose(b16[0:2 * H, t * P:(t + 1) * P],
                                      st.max_parts[:, t, :, :, :].rearrange("p a r j -> p (a r j)"), ident16[:, :])
                mm.then_inc(st.maxT_psum, 1)

            def softmax(st, b):
                def shifted(j):
                    if j >= 2:
                        pe.wait_ge(st.probs_ready, 8 * b + j - 1)
                    for r in range(2):
                        mm = pe.matmul(st.wide[j % 2][0:KEYS, r * S:(r + 1) * S], st.k_stack[:, j, r, :],
                                       st.q_stack[:, j, :], start=True, stop=True)
                    mm.then_inc(st.shifted_psum, 1)

                def weigh(c):
                    bank = (st.bank_a, st.bank_b)[c][:, :].rearrange("p (v s) -> p v s", v=2)
                    for part, src in ((1, None), (0, st.v_cols)):
                        for r in range(2):
                            for n in range(4):
                                j = 4 * c + n
                                if src is None:
                                    pe.wait_ge(st.probs_ready, 8 * b + j + 1)
                                lhs = ones_head[:, r, :] if src is None else src[:, j, r, :]
                                mm = pe.matmul(bank[32 * n:32 * n + 32, part, :], lhs, st.probs[:, 2 * j + r, :],
                                               start=(r == 0), stop=(r == 1))
                    mm.then_inc(st.heads_psum, 1)

                pe.wait_ge(st.max_stacked, 16 * (b + 1))
                pe.wait_ge(st.max_ready, 8 * (b + 1))
                for j in range(6):
                    shifted(j)
                pe.wait_ge(st.maxT_ready, b + 1)
                pe.wait_ge(s_pad, 2)
                weigh(0)
                shifted(6)
                shifted(7)
                weigh(1)

            def attn_out(st, b):
                wo = weights[st.layer][3]
                pe.wait_ge(st.heads_ready, 2 * (b + 1))
                pe.wait_ge(st.probs_ready, 8 * (b + 1))
                w = st.wide[0][:, :].rearrange("p (t d) -> p t d", t=T)
                for t in range(T):
                    for c in range(C):
                        mm = pe.matmul(w[:, t, :], st.heads_out[:, c, t * P:(t + 1) * P], wo[:, c, :],
                                       start=(c == 0), stop=(c == C - 1))
                mm.then_inc(st.attn_psum, 1)

            def ffn_in(st, b):
                a = st.bank_a[:, :].rearrange("p (c s) -> p c s", c=C)
                turn_tokens(a, xm, s_xm, b).then_inc(st.xn2T_psum, 1)

            def ffn_hidden(st, b):
                pe.wait_ge(s_xqT, b + 1)
                if isinstance(b, int) and b == 0:
                    pe.wait_ge(s_prep_act, 8)
                pe.wait_ge(st.x_attn_ready, T * (b + 1))
                for n in range(2 * T):
                    t, half = n // 2, n % 2
                    if n >= 2:
                        pe.wait_ge(s_hid, 4 * b + n - 1)
                    for k in range(C):
                        mm = pe.matmul(st.wide[half][:, :], xqT[:, k, t * P:(t + 1) * P],
                                       w1T[:, k, half * HALF:(half + 1) * HALF], start=(k == 0), stop=(k == C - 1))
                    mm.then_inc(s_h_psum, 1)

            def ffn_out(st, b):
                for t in range(T):
                    pe.wait_ge(s_hq, b * T + t + 1)
                    bank = (st.bank_a, st.bank_b)[t][:, :].bitcast(BF16)
                    for f in range(FC):
                        mm = pe.transpose(bank[:, f * P:(f + 1) * P], hq[:, t, f * P:(f + 1) * P], identb[:, :])
                    mm.then_inc(s_hqT_psum, 1)
                pe.wait_ge(s_hid, 4 * (b + 1))
                for t in range(T):
                    pe.wait_ge(s_hqT, b * T + t + 1)
                    for f in range(FC):
                        mm = pe.matmul(st.wide[t][:, 0:D], hqT[:, t, f, :], w2T[:, f, :], start=(f == 0), stop=(f == FC - 1))
                    mm.then_inc(s_y_psum, 1)

            def route(st, b):
                a = st.bank_a[:, :].rearrange("p (c s) -> p c s", c=C)
                turn_tokens(a, st.xn2, st.xn2_ready, b).then_inc(st.xn2T_psum, 1)
                pe.wait_ge(s_xe, b + 1)
                for t in range(T):
                    dst = st.bank_b[:, t * E:(t + 1) * E]
                    for c in range(C):
                        pe.matmul(dst, xe[:, c, t * P:(t + 1) * P], rwT[:, c, :], start=(c == 0), stop=False)
                    mm = pe.matmul(dst, ones[0:1, :], rb_sb[:, :], start=False, stop=True)
                mm.then_inc(s_router, 1)

            def experts(st, b):
                pe.wait_ge(s_xe_high, b + 1)
                pe.wait_ge(s_xe_low, b + 1)
                pe.wait_ge(st.x_attn_ready, T * (b + 1))

                def expert_pair(n):
                    t, g = n // 4, n % 4
                    if n >= 2:
                        pe.wait_ge(s_acc, b * ACC_STEPS + acc_after(n - 2))
                    last = None
                    for c in range(C):
                        for xp, w in ((0, ew_high), (0, ew_low), (1, ew_high)):
                            first = c == 0 and last is None
                            last = pe.matmul(st.wide[n % 2][:, :], xe_parts[:, xp, c, t * P:(t + 1) * P],
                                             w[:, c, 2 * g:2 * g + 2, :].rearrange("p e o -> p (e o)"),
                                             start=first, stop=(c == C - 1 and xp == 1))
                    last.then_inc(s_exp_psum, 1)

                expert_pair(0)
                expert_pair(1)
                pe.wait_ge(s_route, ROUTE_STEPS * (b + 1))
                for t in range(T):
                    mm = pe.transpose(st.bank_b[0:E, t * P:(t + 1) * P], mix[:, t, :], ident)
                mm.then_inc(s_mixT_psum, 1)
                pe.wait_ge(s_mixT, b + 1)
                w = st.bank_a[:, :].rearrange("p (t d) -> p t d", t=T)
                for t in range(T):
                    mm = pe.matmul(w[:, t, :], mixT[:, t, :], eb_sb[:, :], start=True, stop=True)
                mm.then_inc(s_bias_psum, 1)
                for n in range(2, 4 * T):
                    expert_pair(n)

            parts = dict(prep_attention=prep_attention, prep_ternary=prep_ternary, prep_experts=prep_experts,
                         ln=ln, qkv=qkv, maxima=maxima, softmax=softmax, attn_out=attn_out, ffn_in=ffn_in,
                         ffn_hidden=ffn_hidden, ffn_out=ffn_out, route=route, experts=experts)

            def run(stage, st, b=None):
                parts[stage](*(() if st is None else (st, b)))

            program(pe, run)

        @block.scalar
        def _(act):
            def prep_attention():
                act.wait_ge(s_cst, 16)
                nc.scalar.activation(ident16[:, :], ident, ACT.Copy).then_inc(s_ident, 1)
                nc.scalar.activation(identb[:, :], ident, ACT.Copy).then_inc(s_ident, 1)
                for n in range(4):
                    act.wait_ge(s_prep, n + 1)
                    nc.scalar.activation(wT[n][:, :, :].rearrange("p k o -> p (k o)"), PREP_BANKS[n][:, :],
                                         ACT.Copy).then_inc(s_prep_act, 1)
                act.wait_ge(s_small, 64)
                nc.scalar.activation(gates[:, :], gates[:, :], ACT.Tanh).then_inc(s_gate, 1)

            def prep_ternary():
                for n in range(4):
                    act.wait_ge(s_prep, 6 + n)
                    src = PREP_BANKS[(5 + n) % 4][:, :].bitcast(BF16)
                    if n < 2:
                        dst = w1T[:, n, :]
                    else:
                        dst = w2T[:, 4 * (n - 2):4 * (n - 1), :].rearrange("p f d -> p (f d)")
                    nc.scalar.activation(dst, src, ACT.Copy).then_inc(s_prep_act, 1)

            def prep_experts():
                act.wait_ge(s_prep, 10)
                nc.scalar.activation(rwT[:, :, :].rearrange("p k e -> p (k e)"), PREP_BANKS[9 % 4][:, 0:C * E],
                                     ACT.Copy).then_inc(s_prep_act, 1)
                for e in range(E):
                    act.wait_ge(s_prep, 11 + e)
                    nc.scalar.activation(ew_high[:, :, e, :],
                                         PREP_BANKS[(10 + e) % 4][:, :].rearrange("p (k o) -> p k o", k=C),
                                         ACT.Copy, scale=WSCALE).then_inc(s_prep_act, 1)

            def ln(st, b):
                act.wait_ge(st.xnT_psum, b + 1)
                before(act, st.q_psum, b, 1)
                nc.scalar.activation(st.xnT[:, :, :].rearrange("p c s -> p (c s)"), st.bank_a[:, :],
                                     ACT.Copy).then_inc(st.xnT_ready, 1)
                act.wait_ge(st.ctxT_psum, b + 1)
                before(act, st.v_psum, b, 1)
                nc.scalar.activation(st.ctxT[:, :, :],
                                     st.bank_b[:, :].rearrange("p (c s) -> p c s", c=C)[:, :, 0:KEYS],
                                     ACT.Copy).then_inc(st.ctxT_ready, 1)

            def qkv(st, b):
                act.wait_ge(st.k_psum, b + 1)
                before(act, st.k_stored, b, 16)
                nc.scalar.activation(st.k_parts[:, 0, :, :],
                                     st.bank_b[:, :].rearrange("p (c s) -> p c s", c=C)[:, :, 0:KEYS],
                                     ACT.Copy, scale=st.scale).then_inc(st.k_high, 1)
                act.wait_ge(st.q_psum, b + 1)
                before(act, st.q_stored, b, 16)
                nc.scalar.activation(st.q_parts[:, 0, :, :].rearrange("p c s -> p (c s)"), st.bank_a[:, :],
                                     ACT.Copy).then_inc(st.q_high, 1)

            def maxima(st, b):
                act.wait_ge(st.maxT_psum, b + 1)
                before(act, st.max_stored, b, 16)
                nc.scalar.activation(st.maxT[:, :], st.bank_b[:, :].bitcast(F16)[0:2 * H, 0:S],
                                     ACT.Copy).then_inc(st.maxT_ready, 1)

            def softmax(st, b):
                before(act, st.heads_psum, b, 2)
                for j in range(PAIRS):
                    act.wait_ge(st.shifted_psum, 8 * b + j + 1)
                    nc.scalar.activation(st.probs[:, 2 * j:2 * j + 2, :].rearrange("p h s -> p (h s)"),
                                         st.wide[j % 2][0:KEYS, :], ACT.Exp).then_inc(st.probs_ready, 1)

            def ffn_in(st, b):
                act.wait_ge(st.xn2T_psum, b + 1)
                before(act, s_h_psum, b, 4)
                nc.scalar.activation(xqT[:, :, :].rearrange("p c s -> p (c s)"), st.bank_a[:, :], ACT.Copy,
                                     bias=-MAGIC).then_inc(s_xqT, 1)

            def ffn_hidden(st, b):
                for t in range(T):
                    act.wait_ge(s_hid, 4 * b + 2 * t + 2)
                    nc.scalar.activation(gel[:, t, :], hid[:, t, :], ACT.Gelu).then_inc(s_gel, 1)
                for t in range(T):
                    act.wait_ge(s_gel, b * T + t + 1)
                    if t == 0:
                        before(act, s_sumsq, b, T)
                    else:
                        act.wait_ge(s_sumsq, b * T + t)
                    nc.scalar.activation(hm[:, t, :], gel[:, t, :], ACT.Square,
                                         accum_out=sumsq[:, t:t + 1]).then_inc(s_sumsq, 1)

            def ffn_out(st, b):
                for t in range(T):
                    act.wait_ge(s_hs, HS_STEPS * b + HS_STEPS)
                    nc.scalar.activation(hm[:, t, :], gel[:, t, :], ACT.Copy, scale=ffs[:, 6, t:t + 1],
                                         bias=MAGIC).then_inc(s_hm, 1)
                for t in range(T):
                    act.wait_ge(s_hqT_psum, b * T + t + 1)
                    bank = (st.bank_a, st.bank_b)[t][:, :].bitcast(BF16)
                    nc.scalar.activation(hqT[:, t, :, :].rearrange("p f s -> p (f s)"), bank,
                                         ACT.Copy).then_inc(s_hqT, 1)

            def route(st, b):
                act.wait_ge(st.xn2T_psum, b + 1)
                before(act, s_router, b, 1)
                nc.scalar.activation(xe[:, :, :].rearrange("p c s -> p (c s)"), st.bank_a[:, :],
                                     ACT.Copy).then_inc(s_xe, 1)
                before(act, s_exp_psum, b, 4 * T)
                nc.scalar.activation(xe_parts[:, 0, :, :].rearrange("p c s -> p (c s)"), st.bank_a[:, :],
                                     ACT.Copy).then_inc(s_xe_high, 1)
                act.wait_ge(s_route, ROUTE_STEPS * b + 3)
                nc.scalar.activation(lexp[:, :, :].rearrange("p t e -> p (t e)"),
                                     ldiff[:, :, :].rearrange("p t e -> p (t e)"), ACT.Exp).then_inc(s_lexp, 1)

            def experts(st, b):
                act.wait_ge(s_mixT_psum, b + 1)
                before(act, s_bias_psum, b, 1)
                nc.scalar.activation(mixT[:, :, :].rearrange("e t p -> e (t p)"), st.bank_b[0:E, 0:S],
                                     ACT.Copy).then_inc(s_mixT, 1)

            parts = dict(prep_attention=prep_attention, prep_ternary=prep_ternary, prep_experts=prep_experts,
                         ln=ln, qkv=qkv, maxima=maxima, softmax=softmax, ffn_in=ffn_in,
                         ffn_hidden=ffn_hidden, ffn_out=ffn_out, route=route, experts=experts)

            def run(stage, st, b=None):
                if stage in parts:
                    parts[stage](*(() if st is None else (st, b)))

            program(act, run)

        @block.vector
        def _(dve):
            V = nc.vector

            def prep_attention():
                for st in (X, Y):
                    V.memset(st.v_cols[:, :, :, :].rearrange("p j r c -> p (j r c)"), 0.0).then_inc(s_zero, 1)
                V.memset(ones_head[:, :, :].rearrange("p r c -> p (r c)"), 0.0).then_inc(s_zero, 1)
                V.memset(minus_half[:, :], -0.5).then_inc(s_rows, 1)
                V.memset(eps[:, :], EPS).then_inc(s_rows, 1)
                for st in (X, Y):
                    V.memset(st.k_pairs[STACK:ROWS, :, :].rearrange("p j k -> p (j k)"), 1.0).then_inc(s_rows, 1)
                V.memset(ones[:, :], 1.0).then_inc(s_pad, 1)
                dve.wait_ge(s_zero, 3)
                V.memset(ones_head[:, 0, 0:HD], 1.0).then_inc(s_zero, 1)
                V.memset(ones_head[:, 1, HD:2 * HD], 1.0).then_inc(s_pad, 1)

            def prep_ternary():
                dve.wait_ge(s_w12, 32)
                for n in range(2):
                    V.tensor_reduce(abs_sum[:, n:n + 1], w12[:, n, :], AX.X, ALU.add,
                                    apply_absolute_value=True).then_inc(s_abs, 1)
                dve.wait_ge(s_prep, 5)
                V.tensor_scalar(w_mean[:, :], PREP_BANKS[0][:, 0:2], 1.0 / (F * D), EPS, ALU.mult,
                                ALU.max).then_inc(s_tern, 1)
                dve.wait_ge(s_tern, 1)
                V.reciprocal(w_inv[:, :], w_mean[:, :]).then_inc(s_tern, 1)
                V.tensor_scalar(w_deq[:, :], w_mean[:, :], 1.0 / 127.0, None, ALU.mult).then_inc(s_tern, 1)
                dve.wait_ge(s_tern, 3)
                for n in range(2):
                    V.tensor_scalar(w12_r[:, n, :], w12[:, n, :], w_inv[:, n:n + 1], MAGIC, ALU.mult,
                                    ALU.add).then_inc(s_abs, 1)
                for n in range(2):
                    dve.wait_ge(s_abs, 3 + n)
                    V.tensor_scalar(w12[:, n, :], w12_r[:, n, :], -MAGIC, 1.0, ALU.add, ALU.min).then_inc(s_tern, 1)
                for n in range(2):
                    dve.wait_ge(s_tern, 4 + n)
                    V.tensor_scalar(w12_t[:, n, :], w12[:, n, :], -1.0, None, ALU.max).then_inc(s_tern, 1)
                dve.wait_ge(s_gate, 1)
                V.tensor_scalar(gate_b2[:, :], b2_sb[:, :], gates[:, 2:3], None, ALU.mult).then_inc(s_abs, 1)

            def prep_experts():
                for e in range(E):
                    dve.wait_ge(s_prep_act, 10 + e)
                    V.scalar_tensor_tensor(ew_low[:, :, e, :],
                                           PREP_BANKS[(10 + e) % 4][:, :].rearrange("p (k o) -> p k o", k=C),
                                           WSCALE, ew_high[:, :, e, :], ALU.mult, ALU.subtract).then_inc(s_prep_low, 1)

            def norm(src, stats, mean_var, rstd, dst, steps, done, b):
                for t in range(T):
                    V.bn_stats(stats[:, t, :], src[:, t, :]).then_inc(steps, 1)
                dve.wait_ge(steps, LN_STEPS * b + T)
                V.tensor_copy(stats_seen[:, :], stats[:, 0, 0:1])
                for t in range(T):
                    V.bn_aggr(mean_var[:, t, :], stats[:, t, :]).then_inc(steps, 1)
                dve.wait_ge(steps, LN_STEPS * b + LN_STEPS)
                for t in range(T):
                    V.tensor_scalar(dst[:, t, :], src[:, t, :], mean_var[:, t, 0:1], rstd[:, t:t + 1],
                                    ALU.subtract, ALU.mult).then_inc(done, 1)

            def ln(st, b):
                dve.wait_ge(st.x_ready, (16 if st is X else T) * (b + 1))
                before(dve, st.xnT_psum, b, 1)
                norm(st.x_in, st.stats, st.mean_var, st.rstd, st.xn, st.stats_ready, st.xn_ready, b)

            def qkv(st, b):
                dve.wait_ge(st.k_high, b + 1)
                V.scalar_tensor_tensor(st.k_parts[:, 1, :, :],
                                       st.bank_b[:, :].rearrange("p (c s) -> p c s", c=C)[:, :, 0:KEYS], st.scale,
                                       st.k_parts[:, 0, :, :], ALU.mult, ALU.subtract).then_inc(st.k_low, 1)
                dve.wait_ge(st.v_psum, b + 1)
                before(dve, st.heads_psum, b, 2)
                v = st.wide[0][0:KEYS, 0:D].rearrange("p (j r d) -> p j r d", j=PAIRS, r=2)
                for r in range(2):
                    V.tensor_copy(st.v_cols[:, :, r, r * HD:(r + 1) * HD], v[:, :, r, :]).then_inc(st.v_ready, 1)
                dve.wait_ge(st.q_high, b + 1)
                V.tensor_tensor(st.q_parts[:, 1, :, :].rearrange("p c s -> p (c s)"), st.bank_a[:, :],
                                st.q_parts[:, 0, :, :].rearrange("p c s -> p (c s)"),
                                ALU.subtract).then_inc(st.q_low, 1)

            def maxima(st, b):
                if isinstance(b, int) and b == 0:
                    dve.wait_ge(s_rows, 4)
                    dve.wait_ge(s_cst, 16)
                before(dve, st.shifted_psum, b, PAIRS)
                dve.wait_ge(st.k_paired, 48 * (b + 1))
                for r in range(2):
                    V.tensor_scalar(st.k_stack[:, :, r, :], st.k_pairs[:, :, :], head_mask[0:ROWS, r:r + 1],
                                    None, ALU.mult).then_inc(st.k_stacked, 1)
                for n in range(8):
                    t, g = n // 4, n % 4
                    dve.wait_ge(st.scores_psum, 8 * b + n + 1)
                    V.tensor_reduce(st.neg_max[:, t, 4 * g:4 * g + 4],
                                    st.wide[n % 2][:, 0:4 * KEYS].rearrange("p (h k) -> p h k", h=4), AX.X, ALU.max,
                                    negate=True).then_inc(st.max_ready, 1)
                dve.wait_ge(st.max_ready, 8 * (b + 1))
                before(dve, st.maxT_psum, b, 1)
                nm = st.neg_max[:, :, :].rearrange("p t (j r) -> p t r j", r=2)
                V.tensor_copy(st.max_parts[:, :, 0, :, :], nm).then_inc(st.max_high, 1)
                dve.wait_ge(st.max_high, b + 1)
                V.tensor_tensor(st.max_parts[:, :, 1, :, :], nm, st.max_parts[:, :, 0, :, :],
                                ALU.subtract).then_inc(st.max_low, 1)

            def softmax(st, b):
                for c in range(C):
                    dve.wait_ge(st.heads_psum, 2 * b + c + 1)
                    bank = (st.bank_a, st.bank_b)[c]
                    V.reciprocal(st.den_inv[:, c, :], bank[:, S:2 * S]).then_inc(st.den_ready, 1)
                    dve.wait_ge(st.den_ready, 2 * b + c + 1)
                    if c == 0:
                        before(dve, st.attn_psum, b, 1)
                    V.tensor_tensor(st.heads_out[:, c, :], bank[:, 0:S], st.den_inv[:, c, :],
                                    ALU.mult).then_inc(st.heads_ready, 1)

            def attn_out(st, b):
                dve.wait_ge(st.attn_psum, b + 1)
                if isinstance(b, int) and b == 0:
                    dve.wait_ge(s_gate, 1)
                g = gates[:, st.layer:st.layer + 1]
                for t in range(T):
                    V.scalar_tensor_tensor(st.x_attn[:, t, :], st.wide[0][:, t * D:(t + 1) * D], g, st.x_in[:, t, :],
                                           ALU.mult, ALU.add).then_inc(st.x_attn_ready, 1)
                dve.wait_ge(st.x_attn_ready, T * (b + 1))

            def ffn_in(st, b):
                norm(st.x_attn, st.stats, st.mean_var2, st.rstd2, st.xn2, st.ln2_stats, st.xn2_ready, b)
                dve.wait_ge(st.xn2_ready, T * (b + 1))
                V.tensor_reduce(absmax[:, :], st.xn2[:, :, :], AX.X, ALU.max,
                                apply_absolute_value=True).then_inc(s_absmax, 1)
                base = FFS_STEPS * b
                V.tensor_tensor(ffs[:, 0, :], st.rstd2[:, :], st.rstd2[:, :], ALU.mult).then_inc(s_ffs, 1)
                dve.wait_ge(s_ffs, base + 1)
                V.tensor_tensor(ffs[:, 3, :], ffs[:, 0, :], st.mean_var2[:, :, 1], ALU.mult).then_inc(s_ffs, 1)
                dve.wait_ge(s_ffs, base + 2)
                V.tensor_scalar(ffs[:, 1, :], ffs[:, 3, :], EPS, None, ALU.add).then_inc(s_ffs, 1)
                dve.wait_ge(s_ffs, base + 4)
                dve.wait_ge(s_absmax, b + 1)
                quantise(absmax, 0, s_ffs, base + 4)
                before(dve, st.xn2T_psum, b, 1)
                for t in range(T):
                    V.tensor_scalar(xm[:, t, :], st.xn2[:, t, :], ffs[:, 6, t:t + 1], MAGIC, ALU.mult,
                                    ALU.add).then_inc(s_xm, 1)

            def quantise(amax, w, steps, base):
                V.tensor_tensor(ffs[:, 3, :], amax[:, :], ffs[:, 2, :], ALU.mult).then_inc(steps, 1)
                dve.wait_ge(steps, base + 1)
                V.tensor_scalar(ffs[:, 4, :], ffs[:, 3, :], EPS, None, ALU.max).then_inc(steps, 1)
                dve.wait_ge(steps, base + 2)
                V.reciprocal(ffs[:, 5, :], ffs[:, 4, :]).then_inc(steps, 1)
                V.tensor_scalar(ffs[:, 7, :], ffs[:, 4, :], w_deq[:, w:w + 1], None, ALU.mult).then_inc(steps, 1)
                dve.wait_ge(steps, base + 4)
                V.scalar_tensor_tensor(ffs[:, 6, :], ffs[:, 5, :], 127.0, ffs[:, 2, :], ALU.mult,
                                       ALU.mult).then_inc(steps, 1)
                dve.wait_ge(steps, base + 5)

            def ffn_hidden(st, b):
                for n in range(2 * T):
                    t, half = n // 2, n % 2
                    dve.wait_ge(s_h_psum, 4 * b + n + 1)
                    if n == 0:
                        before(dve, s_gel, b, T)
                    V.scalar_tensor_tensor(hid[:, t, half * HALF:(half + 1) * HALF], st.wide[half][:, :],
                                           ffs[:, 7, t:t + 1], b1_sb[:, half * HALF:(half + 1) * HALF],
                                           ALU.mult, ALU.add).then_inc(s_hid, 1)
                for t in range(T):
                    dve.wait_ge(s_gel, b * T + t + 1)
                    V.tensor_reduce(hmax[:, t:t + 1], gel[:, t, :], AX.X, ALU.max,
                                    apply_absolute_value=True).then_inc(s_hmax, 1)

            def ffn_out(st, b):
                base = HS_STEPS * b
                dve.wait_ge(s_sumsq, T * (b + 1))
                dve.wait_ge(s_hid, 4 * (b + 1))
                V.tensor_scalar(ffs[:, 1, :], sumsq[:, :], 1.0 / F, EPS, ALU.mult, ALU.add).then_inc(s_hs, 1)
                dve.wait_ge(s_hs, base + 1)
                dve.wait_ge(s_hs, base + 2)
                dve.wait_ge(s_hmax, T * (b + 1))
                quantise(hmax, 1, s_hs, base + 2)
                for t in range(T):
                    dve.wait_ge(s_hm, b * T + t + 1)
                    V.tensor_scalar(hq[:, t, :], hm[:, t, :], -MAGIC, None, ALU.add).then_inc(s_hq, 1)
                before(dve, Y.x_attn_ready, b, T)
                dve.wait_ge(s_x1b, b + 1)
                for t in range(T):
                    dve.wait_ge(s_y_psum, b * T + t + 1)
                    V.tensor_scalar(ffs[:, 0, t:t + 1], ffs[:, 7, t:t + 1], gates[:, 2:3], None,
                                    ALU.mult).then_inc(s_gated, 1)
                    dve.wait_ge(s_gated, b * T + t + 1)
                    V.scalar_tensor_tensor(Y.x_in[:, t, :], st.wide[t][:, 0:D], ffs[:, 0, t:t + 1],
                                           x1b[:, t, :], ALU.mult, ALU.add).then_inc(Y.x_ready, 1)

            def route(st, b):
                norm(st.x_attn, st.stats, st.mean_var2, st.rstd2, st.xn2, st.ln2_stats, st.xn2_ready, b)
                dve.wait_ge(s_xe_high, b + 1)
                before(dve, s_exp_psum, b, 4 * T)
                V.tensor_tensor(xe_parts[:, 1, :, :].rearrange("p c s -> p (c s)"), st.bank_a[:, :],
                                xe_parts[:, 0, :, :].rearrange("p c s -> p (c s)"),
                                ALU.subtract).then_inc(s_xe_low, 1)
                dve.wait_ge(s_router, b + 1)
                base = ROUTE_STEPS * b

                def wide(v):
                    return v[:, :].unsqueeze(2).to_broadcast([P, T, E])

                def step(n, ins):
                    ins.then_inc(s_route, 1)
                    dve.wait_ge(s_route, base + n)

                step(1, V.tensor_copy(logits[:, :, :].rearrange("p t e -> p (t e)"), st.bank_b[:, 0:T * E]))
                step(2, V.tensor_reduce(lmax[:, :], logits[:, :, :], AX.X, ALU.max))
                step(3, V.tensor_tensor(ldiff[:, :, :], logits[:, :, :], wide(lmax), ALU.subtract))
                rank_bc = rank.unsqueeze(1).to_broadcast([P, T, E])
                step(4, V.scalar_tensor_tensor(tie[:, :, :], ldiff[:, :, :], 0.0, rank_bc, ALU.is_ge, ALU.mult))
                step(5, V.tensor_reduce(tmax[:, :], tie[:, :, :], AX.X, ALU.max))
                step(6, V.tensor_tensor(hot[:, :, :], tie[:, :, :], wide(tmax), ALU.is_equal))
                dve.wait_ge(s_lexp, b + 1)
                step(7, V.tensor_reduce(lsum[:, :], lexp[:, :, :], AX.X, ALU.add))
                step(8, V.reciprocal(weight[:, :], lsum[:, :]))
                before(dve, s_mixT_psum, b, 1)
                step(9, V.scalar_tensor_tensor(mix[:, :, :], hot[:, :, :], gates[:, 3:4], wide(weight),
                                               ALU.mult, ALU.mult))
                step(10, V.tensor_scalar(mix_w[:, :, :], mix[:, :, :], 1.0 / WSCALE, None, ALU.mult))

            def experts(st, b):
                base = b * ACC_STEPS
                before(dve, s_out, b, 16)
                dve.wait_ge(s_bias_psum, b + 1)
                for t in range(T):
                    V.tensor_tensor(acc[0][:, t, :], st.bank_a[:, t * D:(t + 1) * D], st.x_attn[:, t, :],
                                    ALU.add).then_inc(s_acc, 1)
                    for e in range(E):
                        n = 4 * t + e // 2
                        dve.wait_ge(s_exp_psum, 8 * b + n + 1)
                        dve.wait_ge(s_acc, base + t * (E + 1) + 1 + e)
                        V.scalar_tensor_tensor(acc[(e + 1) % 2][:, t, :],
                                               st.wide[n % 2][:, (e % 2) * D:(e % 2 + 1) * D], mix_w[:, t, e:e + 1],
                                               acc[e % 2][:, t, :], ALU.mult, ALU.add).then_inc(s_acc, 1)

            parts = dict(prep_attention=prep_attention, prep_ternary=prep_ternary, prep_experts=prep_experts,
                         ln=ln, qkv=qkv, maxima=maxima, softmax=softmax, attn_out=attn_out, ffn_in=ffn_in,
                         ffn_hidden=ffn_hidden, ffn_out=ffn_out, route=route, experts=experts)

            def run(stage, st, b=None):
                parts[stage](*(() if st is None else (st, b)))

            program(dve, run)

        @block.gpsimd
        def _(pool):
            def inv_std(mean_var, rstd, steps, b):
                pool.wait_ge(steps, LN_STEPS * b + 2 * T)
                nc.gpsimd.tensor_tensor(rstd[:, :], mean_var[:, :, 1], eps[:, :], ALU.add).then_inc(steps, 1)
                pool.wait_ge(steps, LN_STEPS * b + 2 * T + 1)
                nc.gpsimd.tensor_tensor(rstd[:, :], rstd[:, :], minus_half[:, :], ALU.pow).then_inc(steps, 1)

            def ln(st, b):
                pool.wait_ge(s_rows, 2)
                inv_std(st.mean_var, st.rstd, st.stats_ready, b)

            def route(st, b):
                inv_std(st.mean_var2, st.rstd2, st.ln2_stats, b)

            def ffn_out(st, b):
                pool.wait_ge(s_hs, HS_STEPS * b + 1)
                nc.gpsimd.tensor_tensor(ffs[:, 2, :], ffs[:, 1, :], minus_half[:, :], ALU.pow).then_inc(s_hs, 1)

            def ffn_in(st, b):
                inv_std(st.mean_var2, st.rstd2, st.ln2_stats, b)
                pool.wait_ge(s_ffs, FFS_STEPS * b + 3)
                nc.gpsimd.tensor_tensor(ffs[:, 2, :], ffs[:, 1, :], minus_half[:, :], ALU.pow).then_inc(s_ffs, 1)
                if isinstance(b, int) and b == 0:
                    pool.wait_ge(s_abs, 5)
                pool.wait_ge(st.x_attn_ready, T * (b + 1))
                before(pool, Y.x_ready, b, T)
                nc.gpsimd.tensor_tensor(x1b[:, :, :], st.x_attn[:, :, :],
                                        gate_b2[:, :].unsqueeze(1).to_broadcast([P, T, D]),
                                        ALU.add).then_inc(s_x1b, 1)

            parts = dict(ln=ln, ffn_in=ffn_in, ffn_out=ffn_out, route=route)

            def run(stage, st, b=None):
                if stage in parts:
                    parts[stage](*(() if st is None else (st, b)))

            program(pool, run)


_INS = ['x', 'ctx_1024', 'g_xattn', 'g_ffn', 'L0_xattn_Wq', 'L0_xattn_Wk', 'L0_xattn_Wv', 'L0_xattn_Wo',
        'L0_ffn_w1', 'L0_ffn_b1', 'L0_ffn_w2', 'L0_ffn_b2', 'L1_xattn_W_q', 'L1_xattn_W_kv', 'L1_xattn_W_proj',
        'L1_ffn_router_w', 'L1_ffn_router_b', 'L1_ffn_expert_w', 'L1_ffn_expert_b']


def _constants():
    import numpy as _np
    cst = _np.zeros((P, P + 2 + E), _np.float32)
    cst[:, 0:P] = _np.eye(P, dtype=_np.float32)
    for r in range(2):
        for row in range(STACK):
            cst[row, P + r] = float((row // HD) % 2 == r)
        for row in range(STACK, ROWS):
            cst[row, P + r] = float(row % 2 == r)
    cst[:, P + 2:] = _np.arange(E, 0, -1, dtype=_np.float32)
    return cst


def kernel(**inputs):
    import numpy as _np
    import concourse.bacc as _bacc
    from concourse import mybir as _mybir
    from concourse.bass_utils import run_bass_kernel_spmd as _run

    nc = _bacc.Bacc("TRN2", target_bir_lowering=False, num_devices=1)
    arrays, args = {}, []
    for name in _INS:
        a = _np.ascontiguousarray(inputs[name])
        arrays[f"in_{name}"] = a
        args.append(nc.dram_tensor(f"in_{name}", a.shape, _mybir.dt.from_np(a.dtype), kind="ExternalInput").ap())
    cst = _constants()
    arrays["in_constants"] = cst
    args.append(nc.dram_tensor("in_constants", cst.shape, F32, kind="ExternalInput").ap())
    args.append(nc.dram_tensor("out_0", (B, S, D), F32, kind="ExternalOutput").ap())
    flamingo_kernel(nc, *args)
    r = _run(nc, [arrays], core_ids=[0])
    return r.results[0]["out_0"]
```

```python
from contextlib import ExitStack

import concourse.bass as bass
from concourse import mybir

F32 = mybir.dt.float32
F16 = mybir.dt.float16
BF16 = mybir.dt.bfloat16
ALU = mybir.AluOpType
ACT = mybir.ActivationFunctionType
AX = mybir.AxisListType

P = 128
B, S, D = 8, 256, 256
T = S // P
C = D // P
KEYS = 77
H, HD = 16, 16
PAIRS = H // 2
F = 1024
FC = F // P
E = 8
HALF = 512
STACK = 3 * 2 * HD
ROWS = STACK + 4
EPS = 1e-5
MAGIC = 12582912.0
WSCALE = 1024.0
SCALES = (0.25, 4.0)


def before(eng, sem, b, per):
    if not (isinstance(b, int) and b == 0):
        eng.wait_ge(sem, b * per)


ATTENTION = ("load ctx stats ln turn kv k_load q q_load k_stack max0 max1 max_turn max_rows "
             "soft0 soft1 soft2 soft3 weigh0 weigh1 token0 token1 head_turn attn_out").split()
FEED_FORWARD = ("ff_stats ff_norm ff_scale ff_turn hid0 hid1 hmax0 hmax1 hid_sums hid_scale hq0 hq1 "
                "hq_turn0 hq_turn1 ff_out0 ff_out1").split()
EXPERTS = "ex_stats ex_norm ex_turn router mix_turn bias ex0 ex1 ex2 ex3 ex4 ex5 ex6 ex7".split()
LEADS = dict(A=3, F=2, B=1, E=0)
START = dict(A=1, F=0, B=2, E=1)
MERGE = dict(
    SP="FAAAEBFBEABAAEABAEAAABAAEEFAAAEEAEEEBAFAAFBBEFBBEAFFAABFBBAFBFBFFBFBBBFEBBFBBB",
    PE="BEEAAAAAAEABBBBFAFFBFAEFBBEFEAEAEABABABEBFABFEFABEFBABEFBFBEBBAAFBAAEFBAFAFABB",
    ACT="AAFFBEABEAAEAAFBBBABAFAABEEFBFBAABAEEBBFEABAFFBBFBEAEFBBBFEABEAEABFEAAAFBFAFBB",
    DVE="AAEABFEABAAFEAFBABEABBFBFFEAEAEABBBABBEBBBFBEBFFBAEFEEAFABBFAABAFAAAFEBEFBAFAB",
    POOL="AABBAAFABABFFAFABFABBBFEAAAAFBEBEBAEEFBFABEAEBFBFFBEBFBBFFBBEFEAEEEEBAABAAAAAB")


def order(x, y, merge):
    chains = {"A": (x, ATTENTION), "F": (x, FEED_FORWARD), "B": (y, ATTENTION), "E": (y, EXPERTS)}
    stages = {c: [(s, st, LEADS[c]) for s in names[START[c]:]] + [(s, st, LEADS[c] + 1) for s in names[:START[c]]]
              for c, (st, names) in chains.items()}
    return [stages[c].pop(0) for c in merge]


class Stream:

    def __init__(self, ctx, nc, name, layer, probs=None):
        def sb(n, shape, dt=F32):
            return ctx.enter_context(nc.sbuf_tensor(f"{name}_{n}", shape, dt))

        def sem(n):
            return ctx.enter_context(nc.semaphore(f"{name}_{n}"))

        self.layer = layer
        self.scale = SCALES[layer]
        self.att, self.post = ([ctx.enter_context(nc.psum_tensor(f"{name}_{n}{i}", [P, HALF], F32))
                                for i in range(2)] for n in ("att", "post"))
        self.x_in = sb("x_in", [P, T, D])
        self.residual = sb("residual", [P, T, D]) if layer == 0 else self.x_in
        self.ctx_in = sb("ctx_in", [KEYS, D])
        self.stats = sb("stats", [P, T, 6])
        self.mean_var = sb("mean_var", [P, T, 2])
        self.var_eps = sb("var_eps", [P, T])
        self.rstd = sb("rstd", [P, T])
        self.xn = sb("xn", [P, T, D])
        self.xnT = sb("xnT", [P, C, S])
        self.ctxT = sb("ctxT", [P, C, KEYS])
        self.q_parts = sb("q_parts", [P, 2, C, S], F16)
        self.k_parts = sb("k_parts", [P, 2, C, KEYS], F16)
        self.q_stack = sb("q_stack", [ROWS, PAIRS, S], F16)
        self.k_pairs = sb("k_pairs", [ROWS, PAIRS, KEYS], F16)
        self.k_stack = sb("k_stack", [ROWS, PAIRS, 2, KEYS], F16)
        self.v_cols = sb("v_cols", [KEYS, H, 32])
        self.neg_max = sb("neg_max", [P, T, H])
        self.max_parts = sb("max_parts", [P, T, PAIRS, 2, 2], F16)
        self.probs = sb("probs", [KEYS, H, S]) if probs is None else probs
        self.weighed = sb("weighed", [P, 4, S])
        self.den_inv = sb("den_inv", [P, T, H])
        self.heads = sb("heads", [P, T, D])
        self.headsT = sb("headsT", [P, C, S])
        self.x_attn = sb("x_attn", [P, T, D])
        self.q_dram = nc.dram_tensor(f"{name}_q_dram", [2, D, S], F16, kind="Internal").ap()
        self.k_dram = nc.dram_tensor(f"{name}_k_dram", [2, D, KEYS], F16, kind="Internal").ap()
        self.x_ready = sem("x_ready")
        self.residual_ready = sem("residual_ready")
        self.ctx_ready = sem("ctx_ready")
        self.stats_ready = sem("stats_ready")
        self.xn_ready = sem("xn_ready")
        self.xnT_psum = sem("xnT_psum")
        self.xnT_ready = sem("xnT_ready")
        self.ctxT_psum = sem("ctxT_psum")
        self.ctxT_ready = sem("ctxT_ready")
        self.q_psum = sem("q_psum")
        self.kv_psum = sem("kv_psum")
        self.q_high = sem("q_high")
        self.q_low = sem("q_low")
        self.k_high = sem("k_high")
        self.k_low = sem("k_low")
        self.v_ready = sem("v_ready")
        self.q_stored = sem("q_stored")
        self.k_stored = sem("k_stored")
        self.q_stacked = sem("q_stacked")
        self.k_paired = sem("k_paired")
        self.k_stacked = sem("k_stacked")
        self.scores_psum = sem("scores_psum")
        self.max_ready = sem("max_ready")
        self.max_high = sem("max_high")
        self.max_low = sem("max_low")
        self.max_rows_psum = sem("max_rows_psum")
        self.max_rows0 = sem("max_rows0")
        self.max_rows1 = sem("max_rows1")
        self.shifted_psum = sem("shifted_psum")
        self.probs_ready = sem("probs_ready")
        self.weighed_psum = sem("weighed_psum")
        self.weighed_ready = sem("weighed_ready")
        self.heads_psum = sem("heads_psum")
        self.den_ready = sem("den_ready")
        self.heads_ready = sem("heads_ready")
        self.headsT_psum = sem("headsT_psum")
        self.headsT_ready = sem("headsT_ready")
        self.attn_psum = sem("attn_psum")
        self.x_attn_ready = sem("x_attn_ready")
        self.ln2_stats = sem("ln2_stats")
        self.xn2_ready = sem("xn2_ready")
        self.xn2T_psum = sem("xn2T_psum")
        self.mean_var2 = sb("mean_var2", [P, T, 2])
        self.var_eps2 = sb("var_eps2", [P, T])
        self.rstd2 = sb("rstd2", [P, T])
        self.xn2 = sb("xn2", [P, T, D])


PREPARE = {("stats", 0): "prep_attention", ("max0", 0): "prep_ternary", ("soft0", 0): "prep_experts"}


def flamingo_kernel(nc, x, ctx_tokens, g_xattn, g_ffn, wq0, wk0, wv0, wo0, w1, b1, w2, b2,
                    wq1, wkv1, wproj1, router_w, router_b, expert_w, expert_b, consts, out):
    ctx = ExitStack()
    with ctx:
        def sb(n, shape, dt=F32):
            return ctx.enter_context(nc.sbuf_tensor(n, shape, dt))

        def sem(n):
            return ctx.enter_context(nc.semaphore(n))

        X = Stream(ctx, nc, "x", 0)
        ew_nat = sb("ew_nat", [P, E, C, D])
        Y = Stream(ctx, nc, "y", 1, ew_nat[0:KEYS, :, :, :].rearrange("p e k d -> p (e k) d"))

        cst = sb("cst", [P, P + 2 + E])
        ident = cst[:, 0:P]
        head_mask = cst[:, P:P + 2]
        rank = cst[:, P + 2:P + 2 + E]
        ident16 = sb("ident16", [P, P], F16)
        identb = sb("identb", [P, P], BF16)
        ones = sb("ones", [P, P])
        minus_half = sb("minus_half", [P, 2 * T])
        stats_seen = sb("stats_seen", [P, 1])
        gates = sb("gates", [P, 4])
        nat = [sb(f"nat{i}", [P, C, D]) for i in range(4)]
        wT = [sb(f"wT{i}", [P, C, D]) for i in range(4)]
        wq1_sb = sb("wq1_sb", [P, C, D])
        wkv1_sb = sb("wkv1_sb", [P, C, 2 * D])
        wproj1_sb = sb("wproj1_sb", [P, C, D])
        w12 = sb("w12", [P, 2, FC * D])
        w12_r = sb("w12_r", [P, 2, FC * D])
        w12_t = sb("w12_t", [P, 2, FC * D], BF16)
        w1T = sb("w1T", [P, C, F], BF16)
        w2T = sb("w2T", [P, FC, D], BF16)
        abs_sum = sb("abs_sum", [P, 2])
        w_mean = sb("w_mean", [P, 2])
        w_inv = sb("w_inv", [P, 2])
        w_deq = sb("w_deq", [P, 2])
        gate_b2 = sb("gate_b2", [P, D])
        b1_sb = sb("b1_sb", [P, F])
        b2_sb = sb("b2_sb", [P, D])
        ew_high = sb("ew_high", [P, C, E, D], F16)
        ew_low = sb("ew_low", [P, C, E, D], F16)
        rw_nat = sb("rw_nat", [E, D])
        rwT = sb("rwT", [P, C, E])
        rb_sb = sb("rb_sb", [1, E])
        eb_sb = sb("eb_sb", [E, D])
        absmax = sb("absmax", [P, T])
        ffs = sb("ffs", [P, 8, T])
        xm = sb("xm", [P, T, D])
        xqT = sb("xqT", [P, C, S], BF16)
        hid = w12_r[:, 0, :].rearrange("p (t f) -> p t f", t=T)
        gel = w12_r[:, 1, :].rearrange("p (t f) -> p t f", t=T)
        sumsq = sb("sumsq", [P, T])
        hmax = sb("hmax", [P, T])
        hm = w12[:, 0, :].rearrange("p (t f) -> p t f", t=T)
        hq = w12_t[:, 0, :].rearrange("p (t f) -> p t f", t=T)
        hqT = w12_t[:, 1, :].rearrange("p (t f s) -> p t f s", t=T, f=FC)
        x1b = nat[3]
        xe = nat[2]
        xe_parts = sb("xe_parts", [P, 2, C, S], F16)
        logits = sb("logits", [P, T, E])
        lmax = sb("lmax", [P, T])
        ldiff = sb("ldiff", [P, T, E])
        lexp = sb("lexp", [P, T, E])
        lsum = sb("lsum", [P, T])
        weight = sb("weight", [P, T])
        tie = sb("tie", [P, T, E])
        tmax = sb("tmax", [P, T])
        hot = sb("hot", [P, T, E])
        mix = sb("mix", [P, T, E])
        mix_w = sb("mix_w", [P, T, E])
        mixT = sb("mixT", [E, T, P])
        acc = nat[0:2]

        s_cst, s_attn_w, s_gates_in, s_b1, s_b2, s_w12, s_w1y, s_exp = (
            sem(n) for n in ("cst_loaded", "attn_w_loaded", "gates_loaded", "b1_loaded", "b2_loaded", "w12_loaded",
                             "layer1_loaded", "experts_loaded"))
        s_ident = sem("ident_ready")
        s_fixed = sem("fixed_parts_ready")
        s_gated = sem("ffn_scale_gated")
        s_pad = sem("padding_ready")
        s_gate = sem("gates_ready")
        s_prep = sem("prep_psum")
        s_prep_act = sem("prep_evicted")
        s_prep_low = sem("prep_low")
        s_abs = sem("abs_summed")
        s_tern = sem("ternary_steps")
        s_absmax, s_ffs, s_xm, s_xqT = (sem(n) for n in ("absmax_ready", "ffs_steps", "xm_ready", "xqT_ready"))
        s_h_psum, s_hid, s_gel, s_sumsq, s_hmax, s_hs = (
            sem(n) for n in ("h_psum", "hid_ready", "gelu_ready", "sumsq_ready", "hmax_ready", "h_scale_steps"))
        s_hm, s_hq, s_hqT_psum, s_hqT, s_y_psum, s_x1b = (
            sem(n) for n in ("hm_ready", "hq_ready", "hqT_psum", "hqT_ready", "ffn_psum", "x1b_ready"))
        s_xe, s_xe_high, s_xe_low, s_router, s_route, s_lexp = (
            sem(n) for n in ("xe_ready", "xe_high", "xe_low", "router_psum", "route_steps", "lexp_ready"))
        s_mixT_psum, s_mixT, s_bias_psum, s_exp_psum, s_acc, s_out = (
            sem(n) for n in ("mixT_psum", "mixT_ready", "bias_psum", "expert_psum", "acc_steps", "out_stored"))

        weights = {0: (wT[0], wT[1][:, :, :], wT[2][:, :, :], wT[3]),
                   1: (wq1_sb, wkv1_sb[:, :, 0:D], wkv1_sb[:, :, D:2 * D], wproj1_sb)}

        PREP_BANKS = [*Y.att, *Y.post]
        LN_STEPS = 2 * T + 2
        FFS_STEPS = 9
        HS_STEPS = 7
        ROUTE_STEPS = 10
        FIXED = 5
        ACC_STEPS = T * (E + 1)

        def program(eng, merge, run):
            stages = order(X, Y, MERGE[merge])

            def step(i, skip=False):
                for n, (stage, st, lead) in enumerate(stages):
                    if not skip:
                        run(stage, st, i + lead)
                        continue
                    if st is X and (stage, i + lead) in PREPARE:
                        run(PREPARE[stage, i + lead], None)
                    if 0 <= i + lead < B:
                        run(stage, st, i + lead)

            most = max(lead for _, _, lead in stages)
            for i in range(-most, 1):
                step(i, True)
            with eng.Fori(1, B - most) as i:
                step(i)
            for i in range(B - most, B):
                step(i, True)

        def acc_after(n):
            return T + 2 * n + 2

        block = ctx.enter_context(nc.Block())

        @block.sync
        def _(sp):
            def load_x(b):
                before(sp, X.xn_ready, b, T)
                sp.dma_start(X.x_in[:, :, :], x[b].rearrange("(t p) d -> p t d", p=P)).then_inc(X.x_ready, 16)

            def load_ctx(st, b):
                before(sp, st.ctxT_psum, b, 1)
                sp.dma_start(st.ctx_in[:, :], ctx_tokens[b]).then_inc(st.ctx_ready, 16)

            def natural(dst, src):
                return sp.dma_start(dst, src.rearrange("(k p) n -> p k n", p=P))

            def load_weights():
                sp.dma_start(cst[:, :], consts).then_inc(s_cst, 16)
                load_x(0)
                load_ctx(X, 0)
                for i, w in enumerate((wq0, wk0, wv0, wo0)):
                    natural(nat[i][:, :, :], w).then_inc(s_attn_w, 16)
                sp.dma_start(gates[:, 0:2], g_xattn.partition_broadcast(P)).then_inc(s_gates_in, 16)
                sp.dma_start(gates[:, 2:4], g_ffn.partition_broadcast(P)).then_inc(s_gates_in, 16)
                sp.dma_start(w12[:, 0, :].rearrange("p (k n) -> p k n", k=FC),
                             w1.rearrange("(k p) n -> p k n", p=P)).then_inc(s_w12, 16)
                sp.dma_start(w12[:, 1, :].rearrange("p (k n) -> p k n", k=C),
                             w2.rearrange("(k p) n -> p k n", p=P)).then_inc(s_w12, 16)

            def load_more_weights():
                sp.dma_start(b2_sb[:, :], b2.partition_broadcast(P)).then_inc(s_b2, 16)
                sp.dma_start(rw_nat[:, :], router_w).then_inc(s_exp, 16)
                sp.dma_start(ew_nat[:, :, :, :].rearrange("p e k d -> p (e k) d"),
                             expert_w.rearrange("e (k p) d -> p (e k) d", p=P)).then_inc(s_exp, 16)
                sp.dma_start(b1_sb[:, :], b1.partition_broadcast(P)).then_inc(s_b1, 16)
                natural(wq1_sb[:, :, :], wq1).then_inc(s_w1y, 16)
                natural(wkv1_sb[:, :, :], wkv1).then_inc(s_w1y, 16)
                natural(wproj1_sb[:, :, :], wproj1).then_inc(s_w1y, 16)
                sp.dma_start(rb_sb[:, :], router_b.rearrange("(a e) -> a e", a=1)).then_inc(s_w1y, 16)
                sp.dma_start(eb_sb[:, :], expert_b).then_inc(s_w1y, 16)

            def load(st, b):
                if not (isinstance(b, int) and b == 0 and st is X):
                    load_ctx(st, b)
                    if st is X:
                        load_x(b)

            def kv(st, b):
                sp.wait_ge(st.k_high, b + 1)
                sp.wait_ge(st.k_low, b + 1)
                sp.dma_start(st.k_dram.rearrange("a (c p) k -> p a c k", p=P),
                             st.k_parts[:, :, :, :]).then_inc(st.k_stored, 16)

            def k_load(st, b):
                sp.wait_ge(st.k_stored, 16 * (b + 1))
                for n, part in enumerate((0, 0, 1)):
                    sp.dma_start(st.k_pairs[32 * n:32 * n + 32, :, :],
                                 st.k_dram[part].rearrange("(j r) k -> r j k", r=32)).then_inc(st.k_paired, 16)

            def q(st, b):
                sp.wait_ge(st.q_high, b + 1)
                sp.wait_ge(st.q_low, b + 1)
                sp.dma_start(st.q_dram.rearrange("a (c p) s -> p a c s", p=P),
                             st.q_parts[:, :, :, :]).then_inc(st.q_stored, 16)

            def q_load(st, b):
                if st is X:
                    before(sp, X.x_attn_ready, b, T)
                    sp.dma_start(X.residual[:, :, :],
                                 x[b].rearrange("(t p) d -> p t d", p=P)).then_inc(X.residual_ready, 16)
                sp.wait_ge(st.q_stored, 16 * (b + 1))
                for n, part in enumerate((0, 1, 0)):
                    sp.dma_start(st.q_stack[32 * n:32 * n + 32, :, :],
                                 st.q_dram[part].rearrange("(j r) s -> r j s", r=32)).then_inc(st.q_stacked, 16)

            def ex7(st, b):
                sp.wait_ge(s_acc, b * ACC_STEPS + ACC_STEPS)
                sp.dma_start(out[b].rearrange("(t p) d -> p t d", p=P), acc[0][:, :, :]).then_inc(s_out, 16)

            parts = dict(prep_ternary=load_more_weights, load=load, kv=kv, k_load=k_load, q=q, q_load=q_load, ex7=ex7)
            load_weights()

            def run(stage, st, b=None):
                if stage in parts:
                    parts[stage](*(() if st is None else (st, b)))

            program(sp, "SP", run)
            sp.wait_ge(s_out, 16 * B)

        @block.tensor
        def _(pe):
            def prep_free(n):
                m = n - len(PREP_BANKS)
                if m < 0:
                    return
                if m < 4:
                    pe.wait_ge(s_prep_act, m + 1)
                elif m == 4:
                    pe.wait_ge(s_tern, 1)
                elif m < 10:
                    pe.wait_ge(s_prep_act, m)
                else:
                    pe.wait_ge(s_prep_low, m - 9)

            def prep_attention():
                pe.wait_ge(s_cst, 16)
                pe.wait_ge(s_attn_w, 64)
                for n in range(4):
                    bank = PREP_BANKS[n][:, :].rearrange("p (k o) -> p k o", k=C)
                    for k in range(C):
                        for o in range(C):
                            mm = pe.transpose(bank[:, k, o * P:(o + 1) * P], nat[n][:, o, k * P:(k + 1) * P], ident)
                    mm.then_inc(s_prep, 1)

            def prep_ternary():
                prep_free(4)
                pe.wait_ge(s_abs, 2)
                pe.wait_ge(s_pad, 3)
                pe.matmul(PREP_BANKS[0][:, 0:2], ones[:, :], abs_sum[:, :], start=True, stop=True).then_inc(s_prep, 1)
                pe.wait_ge(s_tern, 7)
                pe.wait_ge(s_ident, 2)
                for n in range(4):
                    prep_free(5 + n)
                    bank = PREP_BANKS[(5 + n) % 4][:, :].bitcast(BF16)
                    for j in range(8):
                        if n < 2:
                            src = w12_t[:, 0, j * D + n * P:j * D + (n + 1) * P]
                        else:
                            f, d = 4 * (n - 2) + j // 2, j % 2
                            src = w12_t[:, 1, d * F + f * P:d * F + (f + 1) * P]
                        mm = pe.transpose(bank[:, j * P:(j + 1) * P], src, identb[:, :])
                    mm.then_inc(s_prep, 1)

            def prep_experts():
                pe.wait_ge(s_exp, 32)
                prep_free(9)
                for k in range(C):
                    mm = pe.transpose(PREP_BANKS[9 % 4][:, k * E:(k + 1) * E], rw_nat[:, k * P:(k + 1) * P],
                                      ident[0:E, 0:E])
                mm.then_inc(s_prep, 1)
                for e in range(E):
                    prep_free(10 + e)
                    bank = PREP_BANKS[(10 + e) % 4][:, :].rearrange("p (k o) -> p k o", k=C)
                    for k in range(C):
                        for o in range(C):
                            mm = pe.transpose(bank[:, k, o * P:(o + 1) * P], ew_nat[:, e, o, k * P:(k + 1) * P], ident)
                    mm.then_inc(s_prep, 1)

            def turn_tokens(dst, src, ready, b):
                for t in range(T):
                    pe.wait_ge(ready, b * T + t + 1)
                    for c in range(C):
                        mm = pe.transpose(dst[:, c, t * P:(t + 1) * P], src[:, t, c * P:(c + 1) * P], ident)
                return mm

            def turn(st, b):
                if st is Y:
                    y_starts(b)
                before(pe, st.headsT_ready, b, 1)
                a = st.att[0][:, :].rearrange("p (c s) -> p c s", c=C)
                turn_tokens(a, st.xn, st.xn_ready, b).then_inc(st.xnT_psum, 1)

            def y_starts(b):
                if isinstance(b, int) and b == 0:
                    pe.wait_ge(s_prep_act, 9 + E)
                    pe.wait_ge(s_prep_low, E)
                    pe.wait_ge(s_w1y, 80)

            def ctx_(st, b):
                if st is Y:
                    y_starts(b)
                elif isinstance(b, int) and b == 0:
                    pe.wait_ge(s_cst, 16)
                before(pe, st.x_attn_ready, b, T)
                pe.wait_ge(st.ctx_ready, 16 * (b + 1))
                bb = st.att[1][:, :].rearrange("p (c s) -> p c s", c=C)
                for c in range(C):
                    mm = pe.transpose(bb[:, c, 0:KEYS], st.ctx_in[:, c * P:(c + 1) * P], ident[0:KEYS, 0:KEYS])
                mm.then_inc(st.ctxT_psum, 1)

            def kv(st, b):
                _, wk, wv, _ = weights[st.layer]
                if st is X and isinstance(b, int) and b == 0:
                    pe.wait_ge(s_prep_act, 4)
                pe.wait_ge(st.ctxT_ready, b + 1)
                for k in range(C):
                    pe.matmul(st.att[1][0:KEYS, D:2 * D], st.ctxT[:, k, :], wv[:, k, :],
                              start=(k == 0), stop=(k == C - 1))
                for o in range(C):
                    for k in range(C):
                        mm = pe.matmul(st.att[1][:, o * KEYS:(o + 1) * KEYS], wk[:, k, o * P:(o + 1) * P],
                                       st.ctxT[:, k, :], start=(k == 0), stop=(k == C - 1))
                mm.then_inc(st.kv_psum, 1)

            def q(st, b):
                wq = weights[st.layer][0]
                a = st.att[0][:, :].rearrange("p (c s) -> p c s", c=C)
                pe.wait_ge(st.xnT_ready, b + 1)
                for o in range(C):
                    for k in range(C):
                        mm = pe.matmul(a[:, o, :], wq[:, k, o * P:(o + 1) * P], st.xnT[:, k, :],
                                       start=(k == 0), stop=(k == C - 1))
                mm.then_inc(st.q_psum, 1)

            def scores(st, b, t):
                if t == 0:
                    pe.wait_ge(st.v_ready, b + 1)
                    pe.wait_ge(st.k_stacked, 2 * (b + 1))
                    pe.wait_ge(st.q_stacked, 48 * (b + 1))
                for g in range(4):
                    n = 4 * t + g
                    if n >= 2:
                        pe.wait_ge(st.max_ready, 8 * b + n - 1)
                    for j in range(2):
                        mm = pe.matmul(st.att[n % 2][:, j * 2 * KEYS:(j + 1) * 2 * KEYS],
                                       st.q_stack[0:STACK, 2 * g + j, t * P:(t + 1) * P],
                                       st.k_stack[0:STACK, 2 * g + j, :, :].rearrange("p r k -> p (r k)"),
                                       start=True, stop=True)
                    mm.then_inc(st.scores_psum, 1)

            def max_turn(st, b):
                pe.wait_ge(st.max_low, b + 1)
                for half in range(2):
                    rows = st.att[half][:, :].bitcast(F16)[STACK:ROWS, :]
                    for n in range(4):
                        for t in range(T):
                            mm = pe.transpose(rows[:, n * S + t * P:n * S + (t + 1) * P],
                                              st.max_parts[:, t, 4 * half + n, :, :].rearrange("p a r -> p (a r)"),
                                              ident16[:, :])
                    mm.then_inc(st.max_rows_psum, 1)

            def shifted(st, b, pairs):
                for j in pairs:
                    if j < 2:
                        pe.wait_ge((st.max_rows0, st.max_rows1)[j], b + 1)
                    if j >= 2:
                        pe.wait_ge(st.probs_ready, 8 * b + j - 1)
                    for r in range(2):
                        mm = pe.matmul(st.att[j % 2][0:KEYS, r * S:(r + 1) * S], st.k_stack[:, j, r, :],
                                       st.q_stack[:, j, :], start=True, stop=True)
                    mm.then_inc(st.shifted_psum, 1)

            def weigh(st, b, half):
                bank = st.att[half][:, :].rearrange("p (g s) -> p g s", g=2)
                if half == 0:
                    if isinstance(b, int) and b == 0:
                        pe.wait_ge(s_pad, 3)
                    pe.wait_ge(st.probs_ready, 8 * b + 7)
                else:
                    pe.wait_ge(st.probs_ready, 8 * b + 8)
                for g in range(2):
                    for n in range(4):
                        h = 8 * half + 4 * g + n
                        mm = pe.matmul(bank[32 * n:32 * n + 32, g, :], st.v_cols[:, h, :], st.probs[:, h, :],
                                       start=True, stop=True)
                mm.then_inc(st.weighed_psum, 1)

            def token(st, b, t):
                pe.wait_ge(st.weighed_ready, 2 * (b + 1))
                for g in range(4):
                    mm = pe.transpose(st.att[t][:, g * P:(g + 1) * P], st.weighed[:, g, t * P:(t + 1) * P], ident)
                mm.then_inc(st.heads_psum, 1)

            def head_turn(st, b):
                a = st.att[0][:, :].rearrange("p (c s) -> p c s", c=C)
                turn_tokens(a, st.heads, st.heads_ready, b).then_inc(st.headsT_psum, 1)

            def attn_out(st, b):
                wo = weights[st.layer][3]
                pe.wait_ge(st.headsT_ready, b + 1)
                w = st.att[1][:, :].rearrange("p (t d) -> p t d", t=T)
                for t in range(T):
                    for c in range(C):
                        mm = pe.matmul(w[:, t, :], st.headsT[:, c, t * P:(t + 1) * P], wo[:, c, :],
                                       start=(c == 0), stop=(c == C - 1))
                mm.then_inc(st.attn_psum, 1)

            def ff_turn(st, b):
                before(pe, Y.x_ready, b, T)
                a = st.post[0][:, :].rearrange("p (c s) -> p c s", c=C)
                turn_tokens(a, xm, s_xm, b).then_inc(st.xn2T_psum, 1)

            def hidden(st, b, t):
                if t == 0:
                    pe.wait_ge(s_xqT, b + 1)
                    if isinstance(b, int) and b == 0:
                        pe.wait_ge(s_prep_act, 8)
                for half in range(2):
                    if t == 1:
                        pe.wait_ge(s_hid, 4 * b + half + 1)
                    for k in range(C):
                        mm = pe.matmul(st.post[half][:, :], xqT[:, k, t * P:(t + 1) * P],
                                       w1T[:, k, half * HALF:(half + 1) * HALF], start=(k == 0), stop=(k == C - 1))
                    mm.then_inc(s_h_psum, 1)

            def hq_turn(st, b, t):
                pe.wait_ge(s_hq, b * T + t + 1)
                bank = st.post[t][:, :].bitcast(BF16)
                for f in range(FC):
                    mm = pe.transpose(bank[:, f * P:(f + 1) * P], hq[:, t, f * P:(f + 1) * P], identb[:, :])
                mm.then_inc(s_hqT_psum, 1)

            def ff_out(st, b, t):
                pe.wait_ge(s_hqT, b * T + t + 1)
                for f in range(FC):
                    mm = pe.matmul(st.post[t][:, 0:D], hqT[:, t, f, :], w2T[:, f, :],
                                   start=(f == 0), stop=(f == FC - 1))
                mm.then_inc(s_y_psum, 1)

            def ex_turn(st, b):
                before(pe, s_acc, b, ACC_STEPS)
                if isinstance(b, int) and b == 0:
                    y_starts(b)
                a = st.post[0][:, :].rearrange("p (c s) -> p c s", c=C)
                turn_tokens(a, st.xn2, st.xn2_ready, b).then_inc(st.xn2T_psum, 1)

            def router(st, b):
                pe.wait_ge(s_xe, b + 1)
                for t in range(T):
                    dst = st.post[1][:, t * E:(t + 1) * E]
                    for c in range(C):
                        pe.matmul(dst, xe[:, c, t * P:(t + 1) * P], rwT[:, c, :], start=(c == 0), stop=False)
                    mm = pe.matmul(dst, ones[0:1, :], rb_sb[:, :], start=False, stop=True)
                mm.then_inc(s_router, 1)

            def mix_turn(st, b):
                pe.wait_ge(s_route, ROUTE_STEPS * (b + 1))
                for t in range(T):
                    mm = pe.transpose(st.post[1][0:E, t * P:(t + 1) * P], mix[:, t, :], ident)
                mm.then_inc(s_mixT_psum, 1)

            def bias(st, b):
                pe.wait_ge(s_mixT, b + 1)
                w = st.post[1][:, :].rearrange("p (t d) -> p t d", t=T)
                for t in range(T):
                    mm = pe.matmul(w[:, t, :], mixT[:, t, :], eb_sb[:, :], start=True, stop=True)
                mm.then_inc(s_bias_psum, 1)

            def expert_pair(st, b, n):
                t, g = n // 4, n % 4
                if n == 0:
                    pe.wait_ge(s_xe_low, b + 1)
                if n == 1:
                    pe.wait_ge(s_acc, b * ACC_STEPS + T)
                if n >= 2:
                    pe.wait_ge(s_acc, b * ACC_STEPS + acc_after(n - 2))
                last = None
                for c in range(C):
                    for xp, w in ((0, ew_high), (0, ew_low), (1, ew_high)):
                        first = c == 0 and last is None
                        last = pe.matmul(st.post[n % 2][:, :], xe_parts[:, xp, c, t * P:(t + 1) * P],
                                         w[:, c, 2 * g:2 * g + 2, :].rearrange("p e o -> p (e o)"),
                                         start=first, stop=(c == C - 1 and xp == 1))
                last.then_inc(s_exp_psum, 1)

            parts = dict(
                prep_attention=prep_attention, prep_ternary=prep_ternary, prep_experts=prep_experts,
                turn=turn, ctx=ctx_, kv=kv, q=q,
                max0=lambda st, b: scores(st, b, 0), max1=lambda st, b: scores(st, b, 1), max_turn=max_turn,
                **{f"soft{n}": lambda st, b, n=n: shifted(st, b, (2 * n, 2 * n + 1)) for n in range(4)},
                weigh0=lambda st, b: weigh(st, b, 0), weigh1=lambda st, b: weigh(st, b, 1),
                token0=lambda st, b: token(st, b, 0), token1=lambda st, b: token(st, b, 1),
                head_turn=head_turn, attn_out=attn_out,
                ff_turn=ff_turn, hid0=lambda st, b: hidden(st, b, 0), hid1=lambda st, b: hidden(st, b, 1),
                hq_turn0=lambda st, b: hq_turn(st, b, 0), hq_turn1=lambda st, b: hq_turn(st, b, 1),
                ff_out0=lambda st, b: ff_out(st, b, 0), ff_out1=lambda st, b: ff_out(st, b, 1),
                ex_turn=ex_turn, router=router, mix_turn=mix_turn, bias=bias,
                **{f"ex{n}": lambda st, b, n=n: expert_pair(st, b, n) for n in range(4 * T)})

            def run(stage, st, b=None):
                if stage in parts:
                    parts[stage](*(() if st is None else (st, b)))

            program(pe, "PE", run)

        @block.scalar
        def _(act):
            def prep_attention():
                act.wait_ge(s_cst, 16)
                nc.scalar.activation(ident16[:, :], ident, ACT.Copy).then_inc(s_ident, 1)
                nc.scalar.activation(identb[:, :], ident, ACT.Copy).then_inc(s_ident, 1)
                for n in range(4):
                    act.wait_ge(s_prep, n + 1)
                    nc.scalar.activation(wT[n][:, :, :].rearrange("p k o -> p (k o)"), PREP_BANKS[n][:, :],
                                         ACT.Copy).then_inc(s_prep_act, 1)
                act.wait_ge(s_gates_in, 32)
                nc.scalar.activation(gates[:, :], gates[:, :], ACT.Tanh).then_inc(s_gate, 1)

            def prep_ternary():
                for n in range(4):
                    act.wait_ge(s_prep, 6 + n)
                    src = PREP_BANKS[(5 + n) % 4][:, :].bitcast(BF16)
                    if n < 2:
                        dst = w1T[:, n, :]
                    else:
                        dst = w2T[:, 4 * (n - 2):4 * (n - 1), :].rearrange("p f d -> p (f d)")
                    nc.scalar.activation(dst, src, ACT.Copy).then_inc(s_prep_act, 1)

            def prep_experts():
                act.wait_ge(s_prep, 10)
                nc.scalar.activation(rwT[:, :, :].rearrange("p k e -> p (k e)"), PREP_BANKS[9 % 4][:, 0:C * E],
                                     ACT.Copy).then_inc(s_prep_act, 1)
                for e in range(E):
                    act.wait_ge(s_prep, 11 + e)
                    nc.scalar.activation(ew_high[:, :, e, :],
                                         PREP_BANKS[(10 + e) % 4][:, :].rearrange("p (k o) -> p k o", k=C),
                                         ACT.Copy, scale=WSCALE).then_inc(s_prep_act, 1)

            def turn(st, b):
                act.wait_ge(st.xnT_psum, b + 1)
                before(act, st.q_psum, b, 1)
                nc.scalar.activation(st.xnT[:, :, :].rearrange("p c s -> p (c s)"), st.att[0][:, :],
                                     ACT.Copy).then_inc(st.xnT_ready, 1)

            def ctx_(st, b):
                act.wait_ge(st.ctxT_psum, b + 1)
                before(act, st.kv_psum, b, 1)
                nc.scalar.activation(st.ctxT[:, :, :],
                                     st.att[1][:, :].rearrange("p (c s) -> p c s", c=C)[:, :, 0:KEYS],
                                     ACT.Copy).then_inc(st.ctxT_ready, 1)

            def kv(st, b):
                act.wait_ge(st.kv_psum, b + 1)
                before(act, st.k_stored, b, 16)
                nc.scalar.activation(st.k_parts[:, 0, :, :],
                                     st.att[1][:, 0:C * KEYS].rearrange("p (c k) -> p c k", c=C),
                                     ACT.Copy, scale=st.scale).then_inc(st.k_high, 1)

            def q(st, b):
                act.wait_ge(st.q_psum, b + 1)
                before(act, st.q_stored, b, 16)
                nc.scalar.activation(st.q_parts[:, 0, :, :].rearrange("p c s -> p (c s)"), st.att[0][:, :],
                                     ACT.Copy).then_inc(st.q_high, 1)

            def max_turn(st, b):
                act.wait_ge(st.max_rows_psum, 2 * b + 1)
                before(act, st.shifted_psum, b, PAIRS)
                nc.scalar.activation(st.q_stack[STACK:ROWS, 0:4, :].rearrange("p j s -> p (j s)"),
                                     st.att[0][:, :].bitcast(F16)[STACK:ROWS, :], ACT.Copy).then_inc(st.max_rows0, 1)

            def soft(st, b, pairs):
                if pairs[0] == 0:
                    before(act, st.weighed_psum, b, 2)
                for j in pairs:
                    act.wait_ge(st.shifted_psum, 8 * b + j + 1)
                    nc.scalar.activation(st.probs[:, 2 * j:2 * j + 2, :].rearrange("p h s -> p (h s)"),
                                         st.att[j % 2][0:KEYS, :], ACT.Exp).then_inc(st.probs_ready, 1)

            def weigh(st, b, half):
                act.wait_ge(st.weighed_psum, 2 * b + half + 1)
                if half == 0:
                    before(act, st.heads_psum, b, T)
                nc.scalar.activation(st.weighed[:, 2 * half:2 * half + 2, :].rearrange("p g s -> p (g s)"),
                                     st.att[half][:, :], ACT.Copy).then_inc(st.weighed_ready, 1)

            def head_turn(st, b):
                act.wait_ge(st.headsT_psum, b + 1)
                before(act, st.attn_psum, b, 1)
                nc.scalar.activation(st.headsT[:, :, :].rearrange("p c s -> p (c s)"), st.att[0][:, :],
                                     ACT.Copy).then_inc(st.headsT_ready, 1)

            def ff_turn(st, b):
                act.wait_ge(st.xn2T_psum, b + 1)
                before(act, s_h_psum, b, 4)
                nc.scalar.activation(xqT[:, :, :].rearrange("p c s -> p (c s)"), st.post[0][:, :], ACT.Copy,
                                     bias=-MAGIC).then_inc(s_xqT, 1)

            def hidden(st, b, t):
                act.wait_ge(s_hid, 4 * b + 2 * t + 2)
                nc.scalar.activation(gel[:, t, :], hid[:, t, :], ACT.Gelu).then_inc(s_gel, 1)
                before(act, s_hq, b, T)
                act.wait_ge(s_gel, b * T + t + 1)
                nc.scalar.activation(hm[:, t, :], gel[:, t, :], ACT.Square,
                                     accum_out=sumsq[:, t:t + 1]).then_inc(s_sumsq, 1)

            def hq(st, b, t):
                act.wait_ge(s_hs, HS_STEPS * b + HS_STEPS)
                nc.scalar.activation(hm[:, t, :], gel[:, t, :], ACT.Copy, scale=ffs[:, 6, t:t + 1],
                                     bias=MAGIC).then_inc(s_hm, 1)

            def hq_turn(st, b, t):
                act.wait_ge(s_hqT_psum, b * T + t + 1)
                bank = st.post[t][:, :].bitcast(BF16)
                nc.scalar.activation(hqT[:, t, :, :].rearrange("p f s -> p (f s)"), bank,
                                     ACT.Copy).then_inc(s_hqT, 1)

            def ex_turn(st, b):
                act.wait_ge(st.xn2T_psum, b + 1)
                before(act, s_router, b, 1)
                nc.scalar.activation(xe[:, :, :].rearrange("p c s -> p (c s)"), st.post[0][:, :],
                                     ACT.Copy).then_inc(s_xe, 1)
                before(act, s_exp_psum, b, 4 * T)
                nc.scalar.activation(xe_parts[:, 0, :, :].rearrange("p c s -> p (c s)"), st.post[0][:, :],
                                     ACT.Copy).then_inc(s_xe_high, 1)

            def router(st, b):
                act.wait_ge(s_route, ROUTE_STEPS * b + 3)
                nc.scalar.activation(lexp[:, :, :].rearrange("p t e -> p (t e)"),
                                     ldiff[:, :, :].rearrange("p t e -> p (t e)"), ACT.Exp).then_inc(s_lexp, 1)

            def mix_turn(st, b):
                act.wait_ge(s_mixT_psum, b + 1)
                before(act, s_bias_psum, b, 1)
                nc.scalar.activation(mixT[:, :, :].rearrange("e t p -> e (t p)"), st.post[1][0:E, 0:S],
                                     ACT.Copy).then_inc(s_mixT, 1)

            parts = dict(
                prep_attention=prep_attention, prep_ternary=prep_ternary, prep_experts=prep_experts,
                turn=turn, ctx=ctx_, kv=kv, q=q, max_turn=max_turn,
                **{f"soft{n}": lambda st, b, n=n: soft(st, b, (2 * n, 2 * n + 1)) for n in range(4)},
                weigh0=lambda st, b: weigh(st, b, 0), weigh1=lambda st, b: weigh(st, b, 1), head_turn=head_turn,
                ff_turn=ff_turn,
                hid0=lambda st, b: hidden(st, b, 0), hid1=lambda st, b: hidden(st, b, 1),
                hq0=lambda st, b: hq(st, b, 0), hq1=lambda st, b: hq(st, b, 1),
                hq_turn0=lambda st, b: hq_turn(st, b, 0), hq_turn1=lambda st, b: hq_turn(st, b, 1),
                ex_turn=ex_turn, router=router, mix_turn=mix_turn)

            def run(stage, st, b=None):
                if stage in parts:
                    parts[stage](*(() if st is None else (st, b)))

            program(act, "ACT", run)

        @block.vector
        def _(dve):
            V = nc.vector

            def prep_attention():
                V.memset(minus_half[:, :], -0.5).then_inc(s_fixed, 1)
                for st in (X, Y):
                    V.memset(st.k_pairs[STACK:ROWS, :, :].rearrange("p j k -> p (j k)"), 1.0).then_inc(s_fixed, 1)
                    V.memset(st.v_cols[:, :, HD + 1:32], 0.0).then_inc(s_fixed, 1)
                    V.memset(st.v_cols[:, :, HD:HD + 1], 1.0).then_inc(s_pad, 1)
                V.memset(ones[:, :], 1.0).then_inc(s_pad, 1)

            def prep_ternary():
                dve.wait_ge(s_w12, 32)
                for n in range(2):
                    V.tensor_reduce(abs_sum[:, n:n + 1], w12[:, n, :], AX.X, ALU.add,
                                    apply_absolute_value=True).then_inc(s_abs, 1)
                dve.wait_ge(s_prep, 5)
                V.tensor_scalar(w_mean[:, :], PREP_BANKS[0][:, 0:2], 1.0 / (F * D), EPS, ALU.mult,
                                ALU.max).then_inc(s_tern, 1)
                dve.wait_ge(s_tern, 1)
                V.reciprocal(w_inv[:, :], w_mean[:, :]).then_inc(s_tern, 1)
                V.tensor_scalar(w_deq[:, :], w_mean[:, :], 1.0 / 127.0, None, ALU.mult).then_inc(s_tern, 1)
                dve.wait_ge(s_tern, 3)
                for n in range(2):
                    V.tensor_scalar(w12_r[:, n, :], w12[:, n, :], w_inv[:, n:n + 1], MAGIC, ALU.mult,
                                    ALU.add).then_inc(s_abs, 1)
                for n in range(2):
                    dve.wait_ge(s_abs, 3 + n)
                    V.tensor_scalar(w12[:, n, :], w12_r[:, n, :], -MAGIC, 1.0, ALU.add, ALU.min).then_inc(s_tern, 1)
                for n in range(2):
                    dve.wait_ge(s_tern, 4 + n)
                    V.tensor_scalar(w12_t[:, n, :], w12[:, n, :], -1.0, None, ALU.max).then_inc(s_tern, 1)

            def prep_experts():
                dve.wait_ge(s_gate, 1)
                dve.wait_ge(s_b2, 16)
                V.tensor_scalar(gate_b2[:, :], b2_sb[:, :], gates[:, 2:3], None, ALU.mult).then_inc(s_abs, 1)
                for e in range(E):
                    dve.wait_ge(s_prep_act, 10 + e)
                    V.scalar_tensor_tensor(ew_low[:, :, e, :],
                                           PREP_BANKS[(10 + e) % 4][:, :].rearrange("p (k o) -> p k o", k=C),
                                           WSCALE, ew_high[:, :, e, :], ALU.mult, ALU.subtract).then_inc(s_prep_low, 1)

            def statistics(src, stats, mean_var, steps, base):
                for t in range(T):
                    V.bn_stats(stats[:, t, :], src[:, t, :]).then_inc(steps, 1)
                dve.wait_ge(steps, base + T)
                V.tensor_copy(stats_seen[:, :], stats[:, 0, 0:1])
                for t in range(T):
                    V.bn_aggr(mean_var[:, t, :], stats[:, t, :]).then_inc(steps, 1)
                dve.wait_ge(steps, base + 2 * T)

            def normalise(src, mean_var, rstd, dst, done):
                for t in range(T):
                    V.tensor_scalar(dst[:, t, :], src[:, t, :], mean_var[:, t, 0:1], rstd[:, t:t + 1],
                                    ALU.subtract, ALU.mult).then_inc(done, 1)

            def stats(st, b):
                dve.wait_ge(st.x_ready, (16 if st is X else T) * (b + 1))
                statistics(st.x_in, st.stats, st.mean_var, st.stats_ready, LN_STEPS * b)
                V.tensor_scalar(st.var_eps[:, :], st.mean_var[:, :, 1], EPS, None, ALU.add).then_inc(st.stats_ready, 1)

            def ln(st, b):
                before(dve, st.xnT_psum, b, 1)
                dve.wait_ge(st.stats_ready, LN_STEPS * (b + 1))
                normalise(st.x_in, st.mean_var, st.rstd, st.xn, st.xn_ready)

            def kv(st, b):
                dve.wait_ge(st.k_high, b + 1)
                V.scalar_tensor_tensor(st.k_parts[:, 1, :, :],
                                       st.att[1][:, 0:C * KEYS].rearrange("p (c k) -> p c k", c=C), st.scale,
                                       st.k_parts[:, 0, :, :], ALU.mult, ALU.subtract).then_inc(st.k_low, 1)
                before(dve, st.weighed_psum, b, 2)
                V.tensor_copy(st.v_cols[:, :, 0:HD],
                              st.att[1][0:KEYS, D:2 * D].rearrange("p (h d) -> p h d", h=H)).then_inc(st.v_ready, 1)

            def q(st, b):
                dve.wait_ge(st.q_high, b + 1)
                V.tensor_tensor(st.q_parts[:, 1, :, :].rearrange("p c s -> p (c s)"), st.att[0][:, :],
                                st.q_parts[:, 0, :, :].rearrange("p c s -> p (c s)"),
                                ALU.subtract).then_inc(st.q_low, 1)

            def maxima(st, b, t):
                if t == 0:
                    before(dve, st.max_low, b, 1)
                for g in range(4):
                    n = 4 * t + g
                    dve.wait_ge(st.scores_psum, 8 * b + n + 1)
                    V.tensor_reduce(st.neg_max[:, t, 4 * g:4 * g + 4],
                                    st.att[n % 2][:, 0:4 * KEYS].rearrange("p (h k) -> p h k", h=4), AX.X, ALU.max,
                                    negate=True).then_inc(st.max_ready, 1)

            def max_turn(st, b):
                dve.wait_ge(st.max_ready, 8 * (b + 1))
                before(dve, st.max_rows_psum, b, 2)
                nm = st.neg_max[:, :, :].rearrange("p t (j r) -> p t j r", r=2)
                V.tensor_copy(st.max_parts[:, :, :, 0, :], nm).then_inc(st.max_high, 1)
                dve.wait_ge(st.max_high, b + 1)
                V.tensor_tensor(st.max_parts[:, :, :, 1, :], nm, st.max_parts[:, :, :, 0, :],
                                ALU.subtract).then_inc(st.max_low, 1)

            def max_rows(st, b):
                dve.wait_ge(st.max_rows_psum, 2 * (b + 1))
                before(dve, st.shifted_psum, b, PAIRS)
                V.tensor_copy(st.q_stack[STACK:ROWS, 4:8, :].rearrange("p j s -> p (j s)"),
                              st.att[1][:, :].bitcast(F16)[STACK:ROWS, :]).then_inc(st.max_rows1, 1)

            def token(st, b, t):
                dve.wait_ge(st.heads_psum, b * T + t + 1)
                got = st.att[t][:, :].rearrange("p (h d) -> p h d", h=H)
                V.reciprocal(st.den_inv[:, t, :], got[:, :, HD]).then_inc(st.den_ready, 1)
                dve.wait_ge(st.den_ready, b * T + t + 1)
                if t == 0:
                    before(dve, st.headsT_psum, b, 1)
                V.tensor_tensor(st.heads[:, t, :].rearrange("p (h d) -> p h d", h=H), got[:, :, 0:HD],
                                st.den_inv[:, t, :].unsqueeze(2).to_broadcast([P, H, HD]),
                                ALU.mult).then_inc(st.heads_ready, 1)

            def attn_out(st, b):
                dve.wait_ge(st.attn_psum, b + 1)
                if isinstance(b, int) and b == 0:
                    dve.wait_ge(s_gate, 1)
                if st is X:
                    dve.wait_ge(X.residual_ready, 16 * (b + 1))
                    before(dve, s_x1b, b, 1)
                elif not isinstance(b, int) or b > 0:
                    dve.wait_ge(s_acc, (b - 1) * ACC_STEPS + T)
                g = gates[:, st.layer:st.layer + 1]
                for t in range(T):
                    V.scalar_tensor_tensor(st.x_attn[:, t, :], st.att[1][:, t * D:(t + 1) * D], g, st.residual[:, t, :],
                                           ALU.mult, ALU.add).then_inc(st.x_attn_ready, 1)

            def second_statistics(st, b):
                statistics(st.x_attn, st.stats, st.mean_var2, st.ln2_stats, LN_STEPS * b)
                V.tensor_scalar(st.var_eps2[:, :], st.mean_var2[:, :, 1], EPS, None, ALU.add).then_inc(st.ln2_stats, 1)

            def ff_stats(st, b):
                dve.wait_ge(st.x_attn_ready, T * (b + 1))
                second_statistics(st, b)

            def ff_norm(st, b):
                before(dve, s_xm, b, T)
                dve.wait_ge(st.ln2_stats, LN_STEPS * (b + 1))
                base = FFS_STEPS * b
                V.tensor_tensor(ffs[:, 0, :], st.rstd2[:, :], st.rstd2[:, :], ALU.mult).then_inc(s_ffs, 1)
                V.tensor_scalar(st.xn2[:, 0, :], st.x_attn[:, 0, :], st.mean_var2[:, 0, 0:1], st.rstd2[:, 0:1],
                                ALU.subtract, ALU.mult).then_inc(st.xn2_ready, 1)
                dve.wait_ge(s_ffs, base + 1)
                V.tensor_tensor(ffs[:, 3, :], ffs[:, 0, :], st.mean_var2[:, :, 1], ALU.mult).then_inc(s_ffs, 1)
                V.tensor_scalar(st.xn2[:, 1, :], st.x_attn[:, 1, :], st.mean_var2[:, 1, 0:1], st.rstd2[:, 1:2],
                                ALU.subtract, ALU.mult).then_inc(st.xn2_ready, 1)
                dve.wait_ge(s_ffs, base + 2)
                V.tensor_scalar(ffs[:, 1, :], ffs[:, 3, :], EPS, None, ALU.add).then_inc(s_ffs, 1)
                dve.wait_ge(st.xn2_ready, T * (b + 1))
                V.tensor_reduce(absmax[:, :], st.xn2[:, :, :], AX.X, ALU.max,
                                apply_absolute_value=True).then_inc(s_absmax, 1)

            def ff_scale(st, b):
                base = FFS_STEPS * b
                dve.wait_ge(s_ffs, base + 4)
                dve.wait_ge(s_absmax, b + 1)
                quantise(absmax, 0, s_ffs, base + 4)
                dve.wait_ge(s_ffs, base + 9)
                before(dve, st.xn2T_psum, b, 1)
                for t in range(T):
                    V.tensor_scalar(xm[:, t, :], st.xn2[:, t, :], ffs[:, 6, t:t + 1], MAGIC, ALU.mult,
                                    ALU.add).then_inc(s_xm, 1)

            def quantise(amax, w, steps, base):
                V.tensor_tensor(ffs[:, 3, :], amax[:, :], ffs[:, 2, :], ALU.mult).then_inc(steps, 1)
                dve.wait_ge(steps, base + 1)
                V.tensor_scalar(ffs[:, 4, :], ffs[:, 3, :], EPS, None, ALU.max).then_inc(steps, 1)
                dve.wait_ge(steps, base + 2)
                V.reciprocal(ffs[:, 5, :], ffs[:, 4, :]).then_inc(steps, 1)
                V.tensor_scalar(ffs[:, 7, :], ffs[:, 4, :], w_deq[:, w:w + 1], None, ALU.mult).then_inc(steps, 1)
                dve.wait_ge(steps, base + 4)
                V.scalar_tensor_tensor(ffs[:, 6, :], ffs[:, 5, :], 127.0, ffs[:, 2, :], ALU.mult,
                                       ALU.mult).then_inc(steps, 1)

            def hidden(st, b, t):
                for half in range(2):
                    dve.wait_ge(s_h_psum, 4 * b + 2 * t + half + 1)
                    if t == 0 and half == 0:
                        if isinstance(b, int) and b == 0:
                            dve.wait_ge(s_b1, 16)
                        before(dve, s_gel, b, T)
                    V.scalar_tensor_tensor(hid[:, t, half * HALF:(half + 1) * HALF], st.post[half][:, :],
                                           ffs[:, 7, t:t + 1], b1_sb[:, half * HALF:(half + 1) * HALF],
                                           ALU.mult, ALU.add).then_inc(s_hid, 1)

            def hidden_max(st, b, t):
                dve.wait_ge(s_gel, b * T + t + 1)
                V.tensor_reduce(hmax[:, t:t + 1], gel[:, t, :], AX.X, ALU.max,
                                apply_absolute_value=True).then_inc(s_hmax, 1)

            def hid_sums(st, b):
                dve.wait_ge(s_sumsq, T * (b + 1))
                V.tensor_scalar(ffs[:, 1, :], sumsq[:, :], 1.0 / F, EPS, ALU.mult, ALU.add).then_inc(s_hs, 1)

            def hid_scale(st, b):
                base = HS_STEPS * b
                dve.wait_ge(s_hid, 4 * (b + 1))
                dve.wait_ge(s_hs, base + 2)
                dve.wait_ge(s_hmax, T * (b + 1))
                quantise(hmax, 1, s_hs, base + 2)

            def hq_(st, b, t):
                dve.wait_ge(s_hm, b * T + t + 1)
                V.tensor_scalar(hq[:, t, :], hm[:, t, :], -MAGIC, None, ALU.add).then_inc(s_hq, 1)

            def ff_out(st, b, t):
                if t == 0:
                    before(dve, Y.x_attn_ready, b, T)
                    dve.wait_ge(s_x1b, b + 1)
                dve.wait_ge(s_y_psum, b * T + t + 1)
                V.tensor_scalar(ffs[:, 0, t:t + 1], ffs[:, 7, t:t + 1], gates[:, 2:3], None,
                                ALU.mult).then_inc(s_gated, 1)
                dve.wait_ge(s_gated, b * T + t + 1)
                V.scalar_tensor_tensor(Y.x_in[:, t, :], st.post[t][:, 0:D], ffs[:, 0, t:t + 1],
                                       x1b[:, t, :], ALU.mult, ALU.add).then_inc(Y.x_ready, 1)

            def ex_stats(st, b):
                dve.wait_ge(st.x_attn_ready, T * (b + 1))
                second_statistics(st, b)

            def ex_norm(st, b):
                before(dve, st.xn2T_psum, b, 1)
                dve.wait_ge(st.ln2_stats, LN_STEPS * (b + 1))
                normalise(st.x_attn, st.mean_var2, st.rstd2, st.xn2, st.xn2_ready)

            def ex_turn(st, b):
                dve.wait_ge(s_xe_high, b + 1)
                before(dve, s_exp_psum, b, 4 * T)
                V.tensor_tensor(xe_parts[:, 1, :, :].rearrange("p c s -> p (c s)"), st.post[0][:, :],
                                xe_parts[:, 0, :, :].rearrange("p c s -> p (c s)"),
                                ALU.subtract).then_inc(s_xe_low, 1)

            def router(st, b):
                dve.wait_ge(s_router, b + 1)
                base = ROUTE_STEPS * b

                def wide(v):
                    return v[:, :].unsqueeze(2).to_broadcast([P, T, E])

                def step(n, ins):
                    ins.then_inc(s_route, 1)
                    if n < ROUTE_STEPS:
                        dve.wait_ge(s_route, base + n)

                step(1, V.tensor_copy(logits[:, :, :].rearrange("p t e -> p (t e)"), st.post[1][:, 0:T * E]))
                step(2, V.tensor_reduce(lmax[:, :], logits[:, :, :], AX.X, ALU.max))
                step(3, V.tensor_tensor(ldiff[:, :, :], logits[:, :, :], wide(lmax), ALU.subtract))
                rank_bc = rank.unsqueeze(1).to_broadcast([P, T, E])
                step(4, V.scalar_tensor_tensor(tie[:, :, :], ldiff[:, :, :], 0.0, rank_bc, ALU.is_ge, ALU.mult))
                step(5, V.tensor_reduce(tmax[:, :], tie[:, :, :], AX.X, ALU.max))
                step(6, V.tensor_tensor(hot[:, :, :], tie[:, :, :], wide(tmax), ALU.is_equal))
                dve.wait_ge(s_lexp, b + 1)
                step(7, V.tensor_reduce(lsum[:, :], lexp[:, :, :], AX.X, ALU.add))
                step(8, V.reciprocal(weight[:, :], lsum[:, :]))
                before(dve, s_mixT_psum, b, 1)
                step(9, V.scalar_tensor_tensor(mix[:, :, :], hot[:, :, :], gates[:, 3:4], wide(weight),
                                               ALU.mult, ALU.mult))
                step(10, V.tensor_scalar(mix_w[:, :, :], mix[:, :, :], 1.0 / WSCALE, None, ALU.mult))

            def bias(st, b):
                before(dve, s_out, b, 16)
                dve.wait_ge(s_bias_psum, b + 1)
                for t in range(T):
                    V.tensor_tensor(acc[0][:, t, :], st.post[1][:, t * D:(t + 1) * D], st.x_attn[:, t, :],
                                    ALU.add).then_inc(s_acc, 1)

            def expert_pair(st, b, n):
                base = b * ACC_STEPS
                t, g = n // 4, n % 4
                for e in (2 * g, 2 * g + 1):
                    dve.wait_ge(s_exp_psum, 8 * b + n + 1)
                    dve.wait_ge(s_acc, base + T + t * E + e)
                    V.scalar_tensor_tensor(acc[(e + 1) % 2][:, t, :],
                                           st.post[n % 2][:, (e % 2) * D:(e % 2 + 1) * D], mix_w[:, t, e:e + 1],
                                           acc[e % 2][:, t, :], ALU.mult, ALU.add).then_inc(s_acc, 1)

            parts = dict(
                prep_attention=prep_attention, prep_ternary=prep_ternary, prep_experts=prep_experts,
                stats=stats, ln=ln, kv=kv, q=q, max0=lambda st, b: maxima(st, b, 0),
                max1=lambda st, b: maxima(st, b, 1), max_turn=max_turn,
                max_rows=max_rows, token0=lambda st, b: token(st, b, 0),
                token1=lambda st, b: token(st, b, 1), attn_out=attn_out, ff_stats=ff_stats,
                ff_norm=ff_norm, ff_scale=ff_scale, hid_sums=hid_sums,
                hid0=lambda st, b: hidden(st, b, 0), hid1=lambda st, b: hidden(st, b, 1),
                hmax0=lambda st, b: hidden_max(st, b, 0), hmax1=lambda st, b: hidden_max(st, b, 1),
                hid_scale=hid_scale, hq0=lambda st, b: hq_(st, b, 0), hq1=lambda st, b: hq_(st, b, 1),
                ff_out0=lambda st, b: ff_out(st, b, 0), ff_out1=lambda st, b: ff_out(st, b, 1),
                ex_stats=ex_stats, ex_norm=ex_norm, ex_turn=ex_turn, router=router, bias=bias,
                **{f"ex{n}": lambda st, b, n=n: expert_pair(st, b, n) for n in range(4 * T)})

            def run(stage, st, b=None):
                if stage in parts:
                    parts[stage](*(() if st is None else (st, b)))

            program(dve, "DVE", run)

        @block.gpsimd
        def _(pool):
            def root(dst, src, steps, base, n):
                pool.wait_ge(steps, base + n)
                nc.gpsimd.tensor_tensor(dst, src, minus_half[:, 0:src.shape[1]], ALU.pow).then_inc(steps, 1)

            def stats(st, b):
                if isinstance(b, int) and b == 0:
                    pool.wait_ge(s_fixed, 1)
                root(st.rstd[:, :], st.var_eps[:, :], st.stats_ready, LN_STEPS * b, LN_STEPS - 1)

            def k_stack(st, b):
                if isinstance(b, int) and b == 0:
                    pool.wait_ge(s_fixed, FIXED)
                    pool.wait_ge(s_cst, 16)
                before(pool, st.shifted_psum, b, PAIRS)
                pool.wait_ge(st.k_paired, 48 * (b + 1))
                for r in range(2):
                    nc.gpsimd.tensor_tensor(st.k_stack[:, :, r, :], st.k_pairs[:, :, :],
                                            head_mask[0:ROWS, r:r + 1].unsqueeze(2).to_broadcast([ROWS, PAIRS, KEYS]),
                                            ALU.mult).then_inc(st.k_stacked, 1)

            def second_stats(st, b):
                root(st.rstd2[:, :], st.var_eps2[:, :], st.ln2_stats, LN_STEPS * b, LN_STEPS - 1)

            def hid_sums(st, b):
                root(ffs[:, 2, :], ffs[:, 1, :], s_hs, HS_STEPS * b, 1)

            def ff_norm(st, b):
                root(ffs[:, 2, :], ffs[:, 1, :], s_ffs, FFS_STEPS * b, 3)
                if isinstance(b, int) and b == 0:
                    pool.wait_ge(s_abs, 5)
                pool.wait_ge(st.x_attn_ready, T * (b + 1))
                before(pool, Y.x_ready, b, T)
                nc.gpsimd.tensor_tensor(x1b[:, :, :], st.x_attn[:, :, :],
                                        gate_b2[:, :].unsqueeze(1).to_broadcast([P, T, D]),
                                        ALU.add).then_inc(s_x1b, 1)

            parts = dict(stats=stats, k_stack=k_stack, ff_stats=second_stats, ff_norm=ff_norm, hid_sums=hid_sums,
                         ex_stats=second_stats)

            def run(stage, st, b=None):
                if stage in parts:
                    parts[stage](*(() if st is None else (st, b)))

            program(pool, "POOL", run)


_INS = ['x', 'ctx_1024', 'g_xattn', 'g_ffn', 'L0_xattn_Wq', 'L0_xattn_Wk', 'L0_xattn_Wv', 'L0_xattn_Wo',
        'L0_ffn_w1', 'L0_ffn_b1', 'L0_ffn_w2', 'L0_ffn_b2', 'L1_xattn_W_q', 'L1_xattn_W_kv', 'L1_xattn_W_proj',
        'L1_ffn_router_w', 'L1_ffn_router_b', 'L1_ffn_expert_w', 'L1_ffn_expert_b']


def _constants():
    import numpy as _np
    cst = _np.zeros((P, P + 2 + E), _np.float32)
    cst[:, 0:P] = _np.eye(P, dtype=_np.float32)
    for r in range(2):
        for row in range(STACK):
            cst[row, P + r] = float((row // HD) % 2 == r)
        for row in range(STACK, ROWS):
            cst[row, P + r] = float(row % 2 == r)
    cst[:, P + 2:] = _np.arange(E, 0, -1, dtype=_np.float32)
    return cst


def kernel(**inputs):
    import numpy as _np
    import concourse.bacc as _bacc
    from concourse import mybir as _mybir
    from concourse.bass_utils import run_bass_kernel_spmd as _run

    nc = _bacc.Bacc("TRN2", target_bir_lowering=False, num_devices=1)
    arrays, args = {}, []
    for name in _INS:
        a = _np.ascontiguousarray(inputs[name])
        arrays[f"in_{name}"] = a
        args.append(nc.dram_tensor(f"in_{name}", a.shape, _mybir.dt.from_np(a.dtype), kind="ExternalInput").ap())
    cst = _constants()
    arrays["in_constants"] = cst
    args.append(nc.dram_tensor("in_constants", cst.shape, F32, kind="ExternalInput").ap())
    args.append(nc.dram_tensor("out_0", (B, S, D), F32, kind="ExternalOutput").ap())
    flamingo_kernel(nc, *args)
    r = _run(nc, [arrays], core_ids=[0])
    return r.results[0]["out_0"]
```
